# Optimizing a Trainium2 kernel written in Bass

```python
import numpy as np
import jax
import jax.numpy as jnp

def _softmax(x, axis=-1):
    return jax.nn.softmax(x, axis=axis)

def _gelu(x):
    return jax.nn.gelu(x, approximate=True)

def _silu(x):
    return jax.nn.silu(x)

def _sigmoid(x):
    return jax.nn.sigmoid(x)

def _layernorm(x, axis=-1, eps=1e-05):
    m = jnp.mean(x, axis=axis, keepdims=True)
    v = jnp.var(x, axis=axis, keepdims=True)
    return (x - m) / jnp.sqrt(v + eps)

def _scatter_add(tgt, idx, src, axis=0):
    return tgt.at[idx].add(src)

def _segment_sum(src, seg, n):
    return jax.ops.segment_sum(src, seg, n)
kernel_name = 'mk_xattn_ffn_d1_seqx_r8_1e18ba'

def setup_inputs(seed: int=0):
    np.random.seed(seed)
    _w = jnp.asarray

    def _rec_inputs():
        import jax
        import jax.numpy as jnp
        _rk = jax.random.key(seed)
        x = 7.22e-05 + 1 * jax.random.normal(jax.random.fold_in(_rk, 1), (4, 512, 128), jnp.float32)
        _lenS = 512 - jax.random.randint(jax.random.fold_in(_rk, 7), (4,), 0, max(1, 512 // 4) + 1, jnp.int32)
        _lenS2 = 77 - jax.random.randint(jax.random.fold_in(_rk, 8), (4,), 0, max(1, 77 // 4) + 1, jnp.int32)
        _ctx_768P = jax.random.normal(jax.random.fold_in(_rk, 11), (4, 16, 96), jnp.float32)
        _ctx_768c = jax.random.dirichlet(jax.random.fold_in(_rk, 511), 0.3 * jnp.ones((16,), jnp.float32), (4, 77))
        _ctx_768t = jnp.einsum('bsk,bkd->bsd', _ctx_768c, _ctx_768P)
        _ctx_768t = _ctx_768t * jax.lax.rsqrt(jnp.mean(jnp.square(_ctx_768t)) + 1e-12) * 0.953939
        ctx_768 = -0.000191848 + 0.999787 * (_ctx_768t + 0.3 * jax.random.normal(jax.random.fold_in(_rk, 611), (4, 77, 96), jnp.float32))
        return (x, ctx_768)
    x, ctx_768 = _rec_inputs()

    def _L0_xattn_setup():
        import jax, jax.numpy as jnp
        import numpy as np
        N_HEADS = 16
        key = jax.random.key(seed)
        ks = jax.random.split(key, 8)
        b, l, m = (8, 128, 128)
        d_embed, d_cross = (128, 96)
        s_q = 1.0 / np.sqrt(d_embed)
        s_kv = 1.0 / np.sqrt(d_cross)
        return {'x': jax.random.normal(ks[0], (b, l, d_embed), jnp.float32), 'y': jax.random.normal(ks[1], (b, m, d_cross), jnp.float32), 'Wq': jax.random.normal(ks[2], (d_embed, d_embed), jnp.float32) * s_q, 'bq': jax.random.normal(ks[3], (d_embed,), jnp.float32) * 0.01, 'Wkv': jax.random.normal(ks[4], (2 * d_embed, d_cross), jnp.float32) * s_kv, 'bkv': jax.random.normal(ks[5], (2 * d_embed,), jnp.float32) * 0.01, 'Wo': jax.random.normal(ks[6], (d_embed, d_embed), jnp.float32) * s_q, 'bo': jax.random.normal(ks[7], (d_embed,), jnp.float32) * 0.01}
    _L0_xattn_all = _L0_xattn_setup()
    _L0_xattn_in = {k: v for k, v in _L0_xattn_all.items() if k in ('Wq', 'bq', 'Wkv', 'bkv', 'Wo', 'bo')}
    del _L0_xattn_all

    def _L0_ffn_setup():
        import jax, jax.numpy as jnp
        import numpy as np
        B, S, H = (2, 256, 128)
        E, I, K = (8, 512, 2)

        def _moe_forward(x, gate_w, wg, wu, wd):
            b, s, h = x.shape
            x_flat = x.reshape(-1, h)
            logits = x_flat @ gate_w.T
            top_v, top_i = jax.lax.top_k(logits, K)
            probs = jax.nn.softmax(top_v.astype(jnp.float32), axis=-1).astype(logits.dtype)
            one_hot = jax.nn.one_hot(top_i, E, dtype=probs.dtype)
            combine = jnp.einsum('tk,tke->et', probs, one_hot)

            def body(acc, ws):
                wge, wue, wde, we = ws
                hidden = jax.nn.silu(x_flat @ wge.T) * (x_flat @ wue.T)
                return (acc + we[:, None] * (hidden @ wde.T), None)
            out, _ = jax.lax.scan(body, jnp.zeros_like(x_flat), (wg, wu, wd, combine))
            return out.reshape(b, s, h)
        key = jax.random.key(seed)
        ks = jax.random.split(key, 5)
        scale_h = 1.0 / np.sqrt(H)
        scale_i = 1.0 / np.sqrt(I)
        x = jax.random.normal(ks[0], (B, S, H), dtype=jnp.float32)
        gate_w = jax.random.normal(ks[1], (E, H), dtype=jnp.float32) * scale_h
        wg = jax.random.normal(ks[2], (E, I, H), dtype=jnp.float32) * scale_h
        wu = jax.random.normal(ks[3], (E, I, H), dtype=jnp.float32) * scale_h
        wd = jax.random.normal(ks[4], (E, H, I), dtype=jnp.float32) * scale_i
        return {'x': x, 'gate_w': gate_w, 'wg': wg, 'wu': wu, 'wd': wd}
    _L0_ffn_all = _L0_ffn_setup()
    _L0_ffn_in = {k: v for k, v in _L0_ffn_all.items() if k in ('gate_w', 'wg', 'wu', 'wd')}
    del _L0_ffn_all
    return {'x': x, 'ctx_768': ctx_768, 'L0_xattn_Wq': _L0_xattn_in['Wq'], 'L0_xattn_bq': _L0_xattn_in['bq'], 'L0_xattn_Wkv': _L0_xattn_in['Wkv'], 'L0_xattn_bkv': _L0_xattn_in['bkv'], 'L0_xattn_Wo': _L0_xattn_in['Wo'], 'L0_xattn_bo': _L0_xattn_in['bo'], 'L0_ffn_gate_w': _L0_ffn_in['gate_w'], 'L0_ffn_wg': _L0_ffn_in['wg'], 'L0_ffn_wu': _L0_ffn_in['wu'], 'L0_ffn_wd': _L0_ffn_in['wd']}

def reference(x, ctx_768, L0_xattn_Wq, L0_xattn_bq, L0_xattn_Wkv, L0_xattn_bkv, L0_xattn_Wo, L0_xattn_bo, L0_ffn_gate_w, L0_ffn_wg, L0_ffn_wu, L0_ffn_wd):
    import jax
    import jax.numpy as jnp

    def _L0_xattn_ref(x, y, Wq, bq, Wkv, bkv, Wo, bo):
        import jax, jax.numpy as jnp
        import numpy as np
        N_HEADS = 16
        b, l, d = x.shape
        m = y.shape[1]
        h = N_HEADS
        dh = d // h
        q = (jnp.einsum('bld,ed->ble', x, Wq) + bq).reshape(b, l, h, dh)
        kv = (jnp.einsum('bmc,ec->bme', y, Wkv) + bkv).reshape(b, m, h, 2 * dh)
        k, v = (kv[..., :dh], kv[..., dh:])
        scale = 1.0 / jnp.sqrt(jnp.asarray(dh, x.dtype))
        att = jax.nn.softmax(jnp.einsum('blhd,bmhd->blmh', q, k) * scale, axis=2)
        out = jnp.einsum('blmh,bmhd->blhd', att, v).reshape(b, l, d)
        return jnp.einsum('bld,ed->ble', out, Wo) + bo

    def _L0_ffn_ref(x, gate_w, wg, wu, wd):
        import jax, jax.numpy as jnp
        import numpy as np
        B, S, H = (2, 256, 128)
        E, I, K = (8, 512, 2)

        def _moe_forward(x, gate_w, wg, wu, wd):
            b, s, h = x.shape
            x_flat = x.reshape(-1, h)
            logits = x_flat @ gate_w.T
            top_v, top_i = jax.lax.top_k(logits, K)
            probs = jax.nn.softmax(top_v.astype(jnp.float32), axis=-1).astype(logits.dtype)
            one_hot = jax.nn.one_hot(top_i, E, dtype=probs.dtype)
            combine = jnp.einsum('tk,tke->et', probs, one_hot)

            def body(acc, ws):
                wge, wue, wde, we = ws
                hidden = jax.nn.silu(x_flat @ wge.T) * (x_flat @ wue.T)
                return (acc + we[:, None] * (hidden @ wde.T), None)
            out, _ = jax.lax.scan(body, jnp.zeros_like(x_flat), (wg, wu, wd, combine))
            return out.reshape(b, s, h)
        return _moe_forward(x, gate_w, wg, wu, wd)
    x = x + _L0_xattn_ref(_layernorm(x, axis=-1), ctx_768, L0_xattn_Wq, L0_xattn_bq, L0_xattn_Wkv, L0_xattn_bkv, L0_xattn_Wo, L0_xattn_bo)
    x = x + _L0_ffn_ref(_layernorm(x, axis=-1), L0_ffn_gate_w, L0_ffn_wg, L0_ffn_wu, L0_ffn_wd)
    return x

_drawn_inputs = setup_inputs


def setup_inputs(seed=0):
    import zlib

    import numpy as np

    out = dict(_drawn_inputs(seed))
    spreads = {}
    factors = {'L0_xattn_bq': 4.011}
    for name, (base, spread) in spreads.items():
        noise = np.random.default_rng([zlib.crc32(name.encode()), seed]).standard_normal(out[name].shape)
        drawn = base * np.exp(spread * noise) if base else spread * noise
        out[name] = jnp.asarray(drawn.astype(out[name].dtype))
    for name, factor in factors.items():
        out[name] = (out[name] * factor).astype(out[name].dtype)
    return out
```

```python
from contextlib import ExitStack

import concourse.bass as bass
from concourse import mybir

ALU = mybir.AluOpType
ACT = mybir.ActivationFunctionType
F32 = mybir.dt.float32
F32R = mybir.dt.float32r
BF16 = mybir.dt.bfloat16
U32 = mybir.dt.uint32
X = mybir.AxisListType.X

P = 128
B, L, D = 4, 512, 128
LT = L // P
NT = B * LT
M, C = 77, 96
H, DH = 16, 8
G = 4
QD = H // G
E, I, TOPK = 8, 512, 2
IC = I // P
EPS = 1e-5
SCALE = float(DH) ** -0.5

ROW_HI, ROW_LO, ROW_KLO, ROW_MAX = 0, 8, 16, 24

SPAN = B * L + P
TILES = B * L * TOPK // P + E - 1
DUMMY = TILES - B * L * TOPK // P
ROWW = D + 2
RET = B * L * TOPK
LAST = TILES - 1


def xattn_moe(nc, x, ctxT, wq, bq, wk, wv, wo, bo, gateT, wgu, wd, out):
    xg = nc.dram_tensor("xg", (E * SPAN + DUMMY * P, ROWW), F32, kind="Internal").ap()
    yr = nc.dram_tensor("yr", (RET + P, D), F32, kind="Internal").ap()

    with ExitStack() as ctx:
        def sb(name, shape, dt=F32):
            return ctx.enter_context(nc.sbuf_tensor(name, shape, dt))

        def sem(name):
            return ctx.enter_context(nc.semaphore(name))

        tok = sb("tok", [P, 3, B, LT, D])
        xa, xn, xb = tok[:, 0], tok[:, 1], tok[:, 2]
        ctxT_s = sb("ctxT_s", [C + 1, B * M])
        wq_s = sb("wq_s", [D, QD, P])
        bq_s = sb("bq_s", [P, QD])
        wk_s = sb("wk_s", [C + 1, QD, P])
        wv_s = sb("wv_s", [C + 1, D])
        wo_s = sb("wo_s", [D, D])
        bo_s = sb("bo_s", [P, D])
        gateT_s = sb("gateT_s", [D, E])
        wgu_s = sb("wgu_s", [D, E, 2 * I])
        wd_s = sb("wd_s", [P, E, IC * D])

        ident = sb("ident", [P, P])
        before = sb("before", [P, P], BF16)
        ones = sb("ones", [P, P], BF16)
        negpow = sb("negpow", [P, LT])
        q_lo = sb("q_lo", [P, 1])
        k_lo = sb("k_lo", [P, 1])
        lane = sb("lane", [P, E])
        ret_row = sb("ret_row", [P, NT, TOPK])

        stat = sb("stat", [P, LT, 6])
        mv1 = sb("mv1", [P, B, LT, 2])
        ve1 = sb("ve1", [P, B, LT])
        rstd1 = sb("rstd1", [P, B, LT])
        xnT = sb("xnT", [D, 2, L])
        qt = sb("qt", [P, 2, L])
        qr = sb("qr", [P, 2, L], F32R)
        qs = sb("qs", [P, 2, QD, L], F32R)
        kr = sb("kr", [P, QD, B * M], F32R)
        ks = sb("ks", [P, QD, B, G, M], F32R)
        vp = sb("vp", [M, B, 2, 2, G, 32])
        nmx = sb("nmx", [P, 2, LT, G, QD])
        nmh = sb("nmh", [H, 2, L], F32R)
        nml = sb("nml", [H, 2, L], F32R)
        ER = 4
        ex = sb("ex", [M, ER, 2, L])
        osb = sb("osb", [P, 2, L])
        rd = sb("rd", [P, 2, LT, 2 * G])
        an = sb("an", [P, LT, 2, 2 * G, DH])
        anT = sb("anT", [D, L])
        x2 = sb("x2", [P, B, LT, D])
        stat2 = sb("stat2", [P, LT, 6])
        mv2 = sb("mv2", [P, LT, 2])
        ve2 = sb("ve2", [P, LT])
        rstd2 = sb("rstd2", [P, LT])
        xs = sb("xs", [P, NT, TOPK, ROWW])
        yb = xs[:].rearrange("p t k w -> p (t k w)")[:, 0:NT * TOPK * D].rearrange("p (t k d) -> p t k d", k=TOPK, d=D)
        x2T = sb("x2T", [D, L])
        lg = sb("lg", [P, LT, E])
        top = sb("top", [P, LT, 8])
        topi = sb("topi", [P, LT, 8], U32)
        topf = sb("topf", [P, LT, TOPK])
        pick = sb("pick", [P, TOPK, LT, E])
        chosen = sb("chosen", [P, LT, E], BF16)
        gap = sb("gap", [P, LT])
        gexp = sb("gexp", [P, LT])
        gden = sb("gden", [P, LT])
        head = sb("head", [P, E])
        pos = sb("pos", [P, LT, E])
        posk = sb("posk", [P, TOPK, LT, E])
        rowf = sb("rowf", [P, TOPK, LT])
        row = sb("row", [P, NT, TOPK], U32)

        base = sb("base", [P, E])
        steps128 = sb("steps128", [1, NT])
        tile_no = sb("tile_no", [1, TILES])
        count = sb("count", [1, E])
        more = sb("more", [1, E, NT])
        ntile = sb("ntile", [1, E])
        one8 = sb("one8", [1, E])
        tile_end = sb("tile_end", [1, E])
        ended = sb("ended", [1, TILES, E])
        skip = sb("skip", [1, E])
        skipped = sb("skipped", [1, TILES, E])
        expf = sb("expf", [1, TILES])
        blkf = sb("blkf", [1, TILES])
        tile_expert = sb("tile_expert", [1, TILES], U32)
        tile_block = sb("tile_block", [1, TILES], U32)
        pad_at = sb("pad_at", [1, E], U32)
        padrow = sb("padrow", [P, ROWW])
        xt = tok[:, 0].rearrange("p b t d -> p (b t d)")[:, 0:2 * ROWW].rearrange("p (n w) -> p n w", n=2)
        eT = tok[:, 1, 0, 0:2]
        ysb = tok[:, 2, 0, 0:2]
        meta = sb("meta", [P, TILES, 2])
        sg, hid, hT = qt, osb, xnT
        ridx = sb("ridx", [P, 2], U32)

        bank = [ctx.enter_context(nc.psum_tensor(f"bank{n}", [P, 512], F32)) for n in range(4, 8)]
        st = ctx.enter_context(nc.psum_tensor("st", [P, G, 512], F32))
        work = bank[0:2]
        opv = bank[2:4]

        s_x = [sem(f"s_xin{b}") for b in range(B)]
        s_wkv = sem("s_wkv"); s_wqo = sem("s_wqo"); s_moew = sem("s_moew")
        s_id = sem("s_id"); s_cst = sem("s_cst"); s_pool = sem("s_pool")
        s_dve = sem("s_dve")
        s_stat1 = sem("s_stat1"); s_rstd1 = sem("s_rstd1"); s_xn = sem("s_xn"); s_xb = sem("s_xb")
        s_kps = sem("s_kps"); s_ksr = sem("s_ksr"); s_ks = sem("s_ks"); s_kz = sem("s_kz")
        s_vps = sem("s_vps"); s_vp = sem("s_vp")
        s_xT = sem("s_xT"); s_xnT = sem("s_xnT")
        s_q = sem("s_q"); s_qt = sem("s_qt"); s_qs = sem("s_qs")
        s_l = sem("s_l"); s_mx = sem("s_mx"); s_nt = sem("s_nt"); s_nm = sem("s_nm")
        s_nmd = [sem(f"s_nmd{n}") for n in range(2)]
        s_s = sem("s_s"); s_e = sem("s_e"); s_pv = sem("s_pv"); s_osb = sem("s_osb")
        s_ot = sem("s_ot"); s_an = sem("s_an"); s_at = sem("s_at"); s_anT = sem("s_anT")
        s_wo = sem("s_wo"); s_x2 = sem("s_x2"); s_stat2 = sem("s_stat2"); s_rstd2 = sem("s_rstd2")
        s_xs = sem("s_xs"); s_xs1 = sem("s_xs1"); s_x2t = sem("s_x2t"); s_x2T = sem("s_x2T")
        s_g = sem("s_g"); s_lg = sem("s_lg"); s_gap = sem("s_gap"); s_gexp = sem("s_gexp"); s_prob = sem("s_prob")
        s_chosen = sem("s_chosen"); s_rk = sem("s_rk"); s_pos = sem("s_pos"); s_row = sem("s_row")
        s_disp = sem("s_disp"); s_out = sem("s_out")
        s_pad = sem("s_pad"); s_padw = sem("s_padw"); s_tab = sem("s_tab")
        s_ld = [sem(f"s_ld{n}") for n in range(2)]
        s_meta = sem("s_meta")
        s_t = sem("s_t"); s_eT = sem("s_eT"); s_gate = sem("s_gate"); s_up = sem("s_up")
        s_silu = sem("s_silu"); s_hid = sem("s_hid"); s_h = sem("s_h"); s_hT = sem("s_hT")
        s_d = sem("s_d"); s_y = sem("s_y")
        s_ret = [sem(f"s_ret{n}") for n in range(2)]
        s_yb = [sem(f"s_yb{n}") for n in range(B)]
        s_fin = sem("s_fin")

        def before_core(b):
            return [[("X", b)] + [("Q", b, i) for i in range(QD)],
                    [("R", b, lt, i) for lt in range(0, 2) for i in range(QD)],
                    [("R", b, lt, i) for lt in range(2, LT) for i in range(QD)] + [("T", b)],
                    []]

        def after_core(b):
            return [[("O", b, 0), ("O", b, 1)], [("A", b), ("W", b)], [("Y", b), ("G", b)], [("K", b)]]

        steps = [("KP", i) for i in range(QD)] + [("VP", b) for b in range(B)]
        steps += sum(before_core(0), [])
        for b in range(B):
            for i in range(QD):
                steps.append(("S", b, i))
                if b + 1 < B:
                    steps += before_core(b + 1)[i]
                if i:
                    steps.append(("V", b, i - 1))
                if b:
                    steps += after_core(b - 1)[i]
            steps.append(("V", b, QD - 1))
        steps += sum(after_core(B - 1), [])

        reader = {"KP": (s_ksr, lambda i: i + 1), "VP": (s_vp, lambda b: b + 1),
                  "X": (s_xnT, lambda b: b + 1), "Q": (s_qt, lambda b, i: QD * b + i + 1),
                  "R": (s_mx, lambda b, lt, i: NT * b + QD * lt + i + 1), "T": (s_nm, lambda b: b + 1),
                  "O": (s_an, lambda b, h: 2 * b + h + 1), "A": (s_anT, lambda b: b + 1),
                  "W": (s_x2, lambda b: b + 1), "Y": (s_x2T, lambda b: b + 1),
                  "G": (s_lg, lambda b: b + 1), "K": (s_pos, lambda b: b + 1)}
        uses = [s for s in steps if s[0] in reader]
        turn = {s: n for n, s in enumerate(uses)}

        def claim(eng, s):
            n = turn[s]
            if n >= 2:
                who, value = reader[uses[n - 2][0]]
                eng.wait_ge(who, value(*uses[n - 2][1:]))
            return work[n % 2]

        FIRST, STOP = 4, LAST
        assert (STOP - FIRST) % 2 == 0

        def pipeline(eng, step):
            for t in range(-1, FIRST):
                step(t, t)
            with eng.Fori(0, (STOP - FIRST) // 2) as i:
                for c in range(2):
                    step(2 * i + FIRST + c, FIRST + c)
            for t in range(STOP, LAST + 3):
                step(t, t)

        def at_least(eng, s, value):
            if not isinstance(value, int) or value > 0:
                eng.wait_ge(s, value)

        block = ctx.enter_context(nc.Block())

        @block.sync
        def _(sp):
            for dst, src in ((ctxT_s, ctxT), (wk_s, wk), (wv_s, wv)):
                sp.dma_start(dst[:], src).then_inc(s_wkv, 16)
            for b in range(B):
                sp.dma_start(xa[:, b], x[b].rearrange("(t p) d -> p t d", p=P)).then_inc(s_x[b], 16)
            for dst, src in ((wq_s, wq), (bq_s, bq), (wo_s, wo), (bo_s, bo), (gateT_s, gateT)):
                sp.dma_start(dst[:], src).then_inc(s_wqo, 16)
            for e in range(E):
                sp.dma_start(wgu_s[:, e, :], wgu[e]).then_inc(s_moew, 16)
                sp.dma_start(wd_s[:, e, :], wd[e]).then_inc(s_moew, 16)
            for b in range(B):
                sp.wait_ge(s_nm, b + 1)
                for n, part in ((0, nmh), (1, nml)):
                    for g in range(G):
                        r = 32 * g + ROW_MAX + n
                        sp.dma_start(qs[r:r + 1, b % 2, :, :].bitcast(F32),
                                     part[QD * g:QD * g + QD, b % 2, :].bitcast(F32)).then_inc(s_nmd[b % 2], 16)
            sp.wait_ge(s_tab, 1)
            sp.wait_ge(s_pad, 1)
            for e in range(E):
                at = sp.value_load(pad_at[0:1, e:e + 1], min_val=e * SPAN, max_val=e * SPAN + B * L)
                sp.dma_start(xg[bass.ds(at, P), :], padrow[:]).then_inc(s_padw, 16)
            sp.dma_start(xg[E * SPAN:E * SPAN + P * DUMMY, :].rearrange("(n p) w -> p n w", p=P),
                         padrow[:, None, :].to_broadcast([P, DUMMY, ROWW])).then_inc(s_padw, 16)
            sp.wait_ge(s_padw, 16 * (E + 1))
            sp.wait_ge(s_disp, 16 * NT * TOPK)
            blocks = xg.rearrange("(n p) w -> n p w", p=P)

            def load(t, c):
                blk = sp.value_load(tile_block[0:1, bass.ds(t, 1)], min_val=0, max_val=E * SPAN // P + DUMMY - 1)
                at_least(sp, s_t, t - 1)
                at_least(sp, s_meta, t - 1)
                sp.dma_start(xt[:, c % 2, :],
                             blocks[bass.ds(blk, 1)].rearrange("a p w -> (a p) w")).then_inc(s_ld[c % 2], 16)

            load(0, 0)
            load(1, 1)
            with sp.Fori(1, (TILES - 1) // 2) as i:
                for c in range(2):
                    load(2 * i + c, 2 + c)
            load(LAST, LAST)
            for n in range(2):
                sp.wait_ge(s_ret[n], 16 * ((TILES + 1 - n) // 2))
            for b in range(B):
                sp.dma_start(yb[:, LT * b:LT * b + LT].rearrange("p t k d -> p t (k d)"),
                             yr[TOPK * L * b:TOPK * L * (b + 1), :].rearrange("(t p k) d -> p t (k d)", p=P, k=TOPK)).then_inc(s_yb[b], 16)
            for b in range(B):
                sp.wait_ge(s_fin, 2 * b + 2)
                sp.dma_start(out[b].rearrange("(t p) d -> p t d", p=P), x2[:, b]).then_inc(s_out, 16)
            sp.wait_ge(s_out, 16 * B)

        @block.gpsimd
        def _(pool):
            pool.memset(ident[:], 0.0).then_inc(s_pool, 1)
            pool.memset(before[:], 1.0).then_inc(s_pool, 1)
            pool.memset(q_lo[:], 0.0).then_inc(s_pool, 1)
            pool.memset(k_lo[:], 0.0).then_inc(s_pool, 1)
            pool.memset(ks[:].rearrange("p a b c d -> p (a b c d)").bitcast(F32), 0.0).then_inc(s_kz, 1)
            pool.memset(negpow[:], -0.5).then_inc(s_pool, 1)
            pool.wait_ge(s_pool, 5)
            pool.affine_select(out=ident[:], in_=ident[:], compare_op=ALU.not_equal, fill=1.0, base=0,
                               pattern=[[-1, P]], channel_multiplier=1).then_inc(s_id, 1)
            pool.affine_select(out=before[:], in_=before[:], compare_op=ALU.is_gt, fill=0.0, base=0,
                               pattern=[[1, P]], channel_multiplier=-1).then_inc(s_cst, 1)
            done = 5
            for t, first in ((q_lo, ROW_LO), (k_lo, ROW_KLO)):
                for g in range(G):
                    for r in range(DH):
                        ins = pool.affine_select(out=t[:], in_=t[:], compare_op=ALU.not_equal, fill=-1.0,
                                                 base=-(32 * g + first + r), pattern=[[0, 1]], channel_multiplier=1)
                        ins.then_inc(s_pool, 1)
                        done += 1
                        pool.wait_ge(s_pool, done)
            pool.memset(ones[:], 1.0).then_inc(s_cst, 1)
            pool.memset(vp[:], 0.0).then_inc(s_cst, 1)
            pool.iota(lane[:], [[1, E]], base=0, channel_multiplier=0,
                      allow_small_or_imprecise_dtypes=True).then_inc(s_cst, 1)
            pool.iota(head[:], [[SPAN, E]], base=0, channel_multiplier=0,
                      allow_small_or_imprecise_dtypes=True).then_inc(s_cst, 1)
            pool.iota(ret_row[:], [[TOPK * P, NT], [1, TOPK]], base=0, channel_multiplier=TOPK,
                      allow_small_or_imprecise_dtypes=True).then_inc(s_cst, 1)
            pool.memset(padrow[:], 0.0).then_inc(s_pool, 1)
            done += 1
            pool.wait_ge(s_pool, done)
            pool.iota(padrow[:, D + 1:D + 2], [[0, 1]], base=RET, channel_multiplier=1,
                      allow_small_or_imprecise_dtypes=True).then_inc(s_pad, 1)
            pool.iota(base[:], [[SPAN, E]], base=0, channel_multiplier=0,
                      allow_small_or_imprecise_dtypes=True).then_inc(s_cst, 1)
            pool.iota(steps128[:], [[P, NT]], base=0, channel_multiplier=0,
                      allow_small_or_imprecise_dtypes=True).then_inc(s_cst, 1)
            pool.iota(tile_no[:], [[1, TILES]], base=0, channel_multiplier=0,
                      allow_small_or_imprecise_dtypes=True).then_inc(s_cst, 1)
            pool.memset(one8[:], 1.0).then_inc(s_cst, 1)
            for b in range(B):
                pool.wait_ge(s_stat1, b + 1)
                pool.tensor_scalar(ve1[:, b], mv1[:, b, :, 1], EPS, None, ALU.add).then_inc(s_pool, 1)
                done += 1
                pool.wait_ge(s_pool, done)
                pool.tensor_tensor(rstd1[:, b], ve1[:, b], negpow[:], ALU.pow).then_inc(s_rstd1, 1)
            pool.wait_ge(s_wqo, 16 * 5)
            for b in range(B):
                pool.tensor_tensor(xb[:, b], xa[:, b], bo_s[:, None, :].to_broadcast([P, LT, D]), ALU.add).then_inc(s_xb, 1)
            for b in range(B):
                pool.wait_ge(s_stat2, b + 1)
                pool.tensor_scalar(ve2[:], mv2[:, :, 1], EPS, None, ALU.add).then_inc(s_pool, 1)
                done += 1
                pool.wait_ge(s_pool, done)
                if b:
                    pool.wait_ge(s_xs, b)
                pool.tensor_tensor(rstd2[:], ve2[:], negpow[:], ALU.pow).then_inc(s_rstd2, 1)
                pool.wait_ge(s_prob, b + 1)
                pool.wait_ge(s_row, b + 1)
                for t in range(LT * b, LT * b + LT):
                    for k in range(TOPK):
                        pool.indirect_dma_start(out=xg, out_offset=bass.IndirectOffsetOnAxis(ap=row[:, t, k:k + 1], axis=0),
                                                in_=xs[:, t, k, :], in_offset=None).then_inc(s_disp, 16)

            last_row = pool.to_reg(RET - 1)
            def step(t, c):
                if c >= 2:
                    pool.wait_ge(s_y, t - 1)
                    pool.nop(nofuse=True)
                    pool.indirect_dma_start(out=yr, out_offset=bass.IndirectOffsetOnAxis(ap=ridx[:, c % 2:c % 2 + 1], axis=0),
                                            in_=ysb[:, c % 2, :], in_offset=None,
                                            bounds_check=last_row, oob_is_err=False).then_inc(s_ret[c % 2], 16)
            pipeline(pool, step)

        @block.tensor
        def _(pe):
            pe.wait_ge(s_id, 1)
            for s in steps:
                kind = s[0]
                b = s[1]
                if kind in reader:
                    w = claim(pe, s)
                if kind == "KP":
                    i = s[1]
                    pe.wait_ge(s_wkv, 48)
                    nc.tensor.matmul(w[:, 0:B * M], wk_s[:, i, :], ctxT_s[:], start=True, stop=True).then_inc(s_kps, 1)
                elif kind == "VP":
                    nc.tensor.matmul(w[0:M, 0:D], ctxT_s[:, M * b:M * b + M], wv_s[:], start=True, stop=True).then_inc(s_vps, 1)
                elif kind == "X":
                    pe.wait_ge(s_xn, b + 1)
                    for t in range(LT):
                        last = nc.tensor.transpose(w[:, P * t:P * t + P], xn[:, b, t, :], ident[:])
                    last.then_inc(s_xT, 1)
                elif kind == "Q":
                    i = s[2]
                    pe.wait_ge(s_xnT, b + 1)
                    pe.wait_ge(s_wqo, 16 * 5)
                    nc.tensor.matmul(w[:], wq_s[:, i, :], xnT[:, b % 2, :], start=True, stop=True).then_inc(s_q, 1)
                elif kind == "R":
                    lt, i = s[2], s[3]
                    pe.wait_ge(s_qs, QD * b + i + 1)
                    pe.wait_ge(s_ks, QD * G)
                    nc.tensor.matmul(w[:, 0:G * M], qs[:, b % 2, i, P * lt:P * lt + P],
                                     ks[:, i, b].rearrange("p g m -> p (g m)"), start=True, stop=True).then_inc(s_l, 1)
                elif kind == "T":
                    pe.wait_ge(s_mx, NT * (b + 1))
                    for t in range(LT):
                        last = nc.tensor.transpose(w[0:H, P * t:P * t + P],
                                                   nmx[:, b % 2, t].rearrange("p g i -> p (g i)"), ident[:])
                    last.then_inc(s_nt, 1)
                elif kind == "S":
                    i = s[2]
                    pe.wait_ge(s_nmd[b % 2], 16 * 2 * G * (b // 2 + 1))
                    for g in range(G):
                        n = 2 * (QD * b + i) + g // 2
                        if g % 2 == 0 and n >= 2:
                            pe.wait_ge(s_e, n - 1)
                        last = nc.tensor.matmul(st[0:M, g, :], ks[:, i, b, g, :], qs[:, b % 2, i, :], start=True, stop=True)
                        if g % 2:
                            last.then_inc(s_s, 1)
                elif kind == "V":
                    i = s[2]
                    if i == 0:
                        pe.wait_ge(s_vp, B)
                    if i % 2 == 0 and b:
                        pe.wait_ge(s_osb, 2 * (b - 1) + i // 2 + 1)
                    for g in range(G):
                        n = 2 * (QD * b + i) + g // 2
                        if g % 2 == 0:
                            pe.wait_ge(s_e, n + 1)
                        last = nc.tensor.matmul(opv[i // 2][32 * g:32 * g + 32, :], vp[:, b, i // 2, i % 2, g, :],
                                                ex[:, n % ER, g % 2, :], start=(i % 2 == 0), stop=(i % 2 == 1),
                                                tile_position=(0, 32 * g))
                        if g % 2:
                            last.then_inc(s_pv, 1)
                elif kind == "O":
                    hf = s[2]
                    pe.wait_ge(s_osb, 2 * b + hf + 1)
                    for t in range(LT):
                        last = nc.tensor.transpose(w[:, P * t:P * t + P], osb[:, hf, P * t:P * t + P], ident[:])
                    last.then_inc(s_ot, 1)
                elif kind == "A":
                    pe.wait_ge(s_an, 2 * (b + 1))
                    for t in range(LT):
                        last = nc.tensor.transpose(w[:, P * t:P * t + P],
                                                   an[:, t].rearrange("p a b d -> p (a b d)"), ident[:])
                    last.then_inc(s_at, 1)
                elif kind == "W":
                    pe.wait_ge(s_anT, b + 1)
                    for t in range(LT):
                        last = nc.tensor.matmul(w[:, P * t:P * t + P], anT[:, P * t:P * t + P], wo_s[:], start=True, stop=True)
                    last.then_inc(s_wo, 1)
                elif kind == "Y":
                    pe.wait_ge(s_xs, b + 1)
                    for t in range(LT):
                        last = nc.tensor.transpose(w[:, P * t:P * t + P], xs[:, LT * b + t, 0, 0:D], ident[:])
                    last.then_inc(s_x2t, 1)
                elif kind == "G":
                    pe.wait_ge(s_x2T, b + 1)
                    for t in range(LT):
                        last = nc.tensor.matmul(w[:, E * t:E * t + E], x2T[:, P * t:P * t + P], gateT_s[:], start=True, stop=True)
                    last.then_inc(s_g, 1)
                elif kind == "K":
                    pe.wait_ge(s_chosen, b + 1)
                    pe.wait_ge(s_cst, 10)
                    nc.tensor.matmul(w[:, 0:LT * E], before[:], chosen[:].rearrange("p t e -> p (t e)"), start=True, stop=False)
                    for t in range(LT - 1):
                        nc.tensor.matmul(w[:, E * (t + 1):LT * E], ones[:],
                                         chosen[:, t:t + 1, :].to_broadcast([P, LT - 1 - t, E]),
                                         start=False, stop=(t == LT - 2))
                    for t in range(LT):
                        last = nc.tensor.matmul(w[:, LT * E:LT * E + E], ones[:], chosen[:, t, :],
                                                start=(t == 0), stop=(t == LT - 1))
                    last.then_inc(s_rk, 1)

            pe.wait_ge(s_e, 2 * QD * B)
            pe.wait_ge(s_osb, 2 * B)
            pe.wait_ge(s_pos, B)
            pe.wait_ge(s_moew, 16 * 2 * E)
            pe.wait_ge(s_tab, 1)

            def step(t, c):
                if 0 <= c <= LAST:
                    e = pe.value_load(tile_expert[0:1, bass.ds(t, 1)], min_val=0, max_val=E - 1)
                    pe.wait_ge(s_eT, t + 1)
                    at_least(pe, s_silu, t - 1)
                    at_least(pe, s_hid, t - 1)
                    for n, done in ((0, s_gate), (1, s_up)):
                        nc.tensor.matmul(st[:, 2 * n + c % 2, :], eT[:, c % 2, :],
                                         wgu_s[:, bass.ds(e, 1), I * n:I * n + I].rearrange("p a n -> p (a n)"),
                                         start=True, stop=True).then_inc(done, 1)
                if c + 1 <= LAST:
                    pe.wait_ge(s_ld[(c + 1) % 2], 8 * (t + 1 - (c + 1) % 2) + 16)
                    at_least(pe, s_eT, t + 1)
                    nc.tensor.transpose(work[0][:, 0:P], xt[:, (c + 1) % 2, 0:D], ident[:]).then_inc(s_t, 1)
                if 1 <= c <= LAST + 1:
                    pe.wait_ge(s_hid, t)
                    at_least(pe, s_hT, t - 2)
                    for n in range(IC):
                        last = nc.tensor.transpose(opv[(c + 1) % 2][:, P * n:P * n + P], hid[:, (c + 1) % 2, P * n:P * n + P], ident[:])
                    last.then_inc(s_h, 1)
                if c >= 2:
                    e = pe.value_load(tile_expert[0:1, bass.ds(t - 2, 1)], min_val=0, max_val=E - 1)
                    pe.wait_ge(s_hT, t - 1)
                    at_least(pe, s_y, t - 2)
                    for n in range(IC):
                        last = nc.tensor.matmul(work[1][:, 0:D], hT[:, c % 2, P * n:P * n + P],
                                                wd_s[:, bass.ds(e, 1), D * n:D * n + D].rearrange("p a n -> p (a n)"),
                                                start=(n == 0), stop=(n == IC - 1))
                    last.then_inc(s_d, 1)
            pipeline(pe, step)

        @block.scalar
        def _(act):
            for s in steps:
                kind = s[0]
                b = s[1]
                w = work[turn[s] % 2] if s in turn else None
                if kind == "Q":
                    i = s[2]
                    n = QD * b + i
                    act.wait_ge(s_q, n + 1)
                    if n >= 2:
                        act.wait_ge(s_qs, n - 1)
                    nc.scalar.activation(qt[:, n % 2, :], w[:], ACT.Identity, bias=bq_s[:, i:i + 1]).then_inc(s_qt, 1)
                elif kind == "S":
                    i = s[2]
                    for pr in range(2):
                        n = 2 * (QD * b + i) + pr
                        act.wait_ge(s_s, n + 1)
                        if n >= ER:
                            act.wait_ge(s_pv, n - ER + 1)
                        nc.scalar.activation(ex[:, n % ER], st[0:M, 2 * pr:2 * pr + 2, :], ACT.Exp, scale=SCALE).then_inc(s_e, 1)
                elif kind == "V" and s[2] % 2:
                    hf = s[2] // 2
                    act.wait_ge(s_pv, 2 * (QD * b + s[2] + 1))
                    if b:
                        act.wait_ge(s_ot, 2 * (b - 1) + hf + 1)
                    nc.scalar.copy(osb[:, hf, :], opv[hf][:]).then_inc(s_osb, 1)
                elif kind == "A":
                    act.wait_ge(s_at, b + 1)
                    if b:
                        act.wait_ge(s_wo, b)
                    nc.scalar.copy(anT[:], w[:]).then_inc(s_anT, 1)
                elif kind == "Y":
                    act.wait_ge(s_x2t, b + 1)
                    if b:
                        act.wait_ge(s_g, b)
                    nc.scalar.copy(x2T[:], w[:]).then_inc(s_x2T, 1)
                elif kind == "G":
                    act.wait_ge(s_gap, b + 1)
                    nc.scalar.activation(gexp[:], gap[:], ACT.Exp).then_inc(s_gexp, 1)

            def step(t, c):
                if 0 <= c <= LAST:
                    act.wait_ge(s_gate, t + 1)
                    at_least(act, s_hid, t - 1)
                    nc.scalar.activation(sg[:, c % 2, :], st[:, c % 2, :], ACT.Silu).then_inc(s_silu, 1)
                if c + 1 <= LAST:
                    act.wait_ge(s_t, t + 2)
                    at_least(act, s_up, t)
                    nc.scalar.copy(eT[:, (c + 1) % 2, :], work[0][:, 0:P]).then_inc(s_eT, 1)
                if 1 <= c <= LAST + 1:
                    act.wait_ge(s_h, t)
                    at_least(act, s_d, t - 2)
                    nc.scalar.copy(hT[:, (c + 1) % 2, :], opv[(c + 1) % 2][:]).then_inc(s_hT, 1)
            pipeline(act, step)

        @block.vector
        def _(dve):
            chain = [0]

            def link(ins):
                chain[0] += 1
                ins.then_inc(s_dve, 1)
                dve.wait_ge(s_dve, chain[0])

            V = nc.vector

            def stats1(b):
                dve.wait_ge(s_x[b], 16)
                for t in range(LT):
                    ins = V.bn_stats(stat[:, t, :], xa[:, b, t, :])
                link(ins)
                for t in range(LT):
                    ins = V.bn_aggr(mv1[:, b, t, :], stat[:, t, :])
                ins.then_inc(s_stat1, 1)
                dve.wait_ge(s_stat1, b + 1)

            def norm1(b):
                dve.wait_ge(s_rstd1, b + 1)
                for t in range(LT):
                    ins = V.tensor_scalar(xn[:, b, t, :], xa[:, b, t, :], mv1[:, b, t, 0:1], rstd1[:, b, t:t + 1],
                                          ALU.subtract, ALU.mult)
                ins.then_inc(s_xn, 1)

            stats1(0)
            stats1(1)
            norm1(0)
            for s in steps:
                kind = s[0]
                b = s[1]
                w = work[turn[s] % 2] if s in turn else None
                if kind == "KP":
                    i = s[1]
                    dve.wait_ge(s_kps, i + 1)
                    if i == 0:
                        dve.wait_ge(s_kz, 1)
                        dve.wait_ge(s_pool, 5 + 2 * G * DH)
                    link(V.tensor_copy(kr[:, i, :], w[:, 0:B * M]))
                    V.scalar_tensor_tensor(kr[:, i, :], kr[:, i, :].bitcast(F32), k_lo[:, 0:1], w[:, 0:B * M],
                                           ALU.mult, ALU.add).then_inc(s_ksr, 1)
                    dve.wait_ge(s_ksr, i + 1)
                    for g in range(G):
                        r = slice(32 * g, 32 * g + 32)
                        V.tensor_copy(ks[r, i, :, g, :], kr[r, i, :].bitcast(F32).rearrange("p (b m) -> p b m", b=B)).then_inc(s_ks, 1)
                elif kind == "VP":
                    dve.wait_ge(s_vps, b + 1)
                    if b == 0:
                        dve.wait_ge(s_cst, 10)
                    for hf in range(2):
                        for j in range(2):
                            i = 2 * hf + j
                            V.tensor_copy(vp[:, b, hf, j, :, 16 * j:16 * j + DH],
                                          w[0:M, 32 * i:32 * i + 32].rearrange("m (g d) -> m g d", g=G))
                    for j in range(2):
                        ins = V.memset(vp[:, b, :, j, :, 16 * j + DH:16 * j + DH + 1], 1.0)
                    ins.then_inc(s_vp, 1)
                    if b < B - 2:
                        stats1(b + 2)
                    if b < B - 1:
                        norm1(b + 1)
                elif kind == "X":
                    dve.wait_ge(s_xT, b + 1)
                    if b >= 2:
                        dve.wait_ge(s_q, QD * (b - 1))
                    V.tensor_copy(xnT[:, b % 2, :], w[:]).then_inc(s_xnT, 1)
                elif kind == "Q":
                    n = QD * b + s[2]
                    dve.wait_ge(s_qt, n + 1)
                    if b >= 2 and s[2] == 0:
                        dve.wait_ge(s_s, 2 * QD * (b - 1))
                    link(V.tensor_copy(qr[:, n % 2, :], qt[:, n % 2, :]))
                    V.scalar_tensor_tensor(qs[:, b % 2, s[2], :], qr[:, n % 2, :].bitcast(F32), q_lo[:, 0:1],
                                           qt[:, n % 2, :], ALU.mult, ALU.add).then_inc(s_qs, 1)
                elif kind == "R":
                    lt, i = s[2], s[3]
                    n = NT * b + QD * lt + i
                    dve.wait_ge(s_l, n + 1)
                    if b >= 2 and lt == 0 and i == 0:
                        dve.wait_ge(s_nt, b - 1)
                    V.tensor_reduce(nmx[:, b % 2, lt, :, i], w[:, 0:G * M].rearrange("p (g m) -> p g m", g=G),
                                    X, ALU.max, negate=True).then_inc(s_mx, 1)
                elif kind == "T":
                    dve.wait_ge(s_nt, b + 1)
                    if b >= 2:
                        dve.wait_ge(s_nmd[b % 2], 16 * 2 * G * (b // 2))
                    link(V.tensor_copy(nmh[:, b % 2, :], w[0:H, :]))
                    V.scalar_tensor_tensor(nml[:, b % 2, :], nmh[:, b % 2, :].bitcast(F32), -1.0, w[0:H, :],
                                           ALU.mult, ALU.add).then_inc(s_nm, 1)
                elif kind == "O":
                    hf = s[2]
                    dve.wait_ge(s_ot, 2 * b + hf + 1)
                    if b and hf == 0:
                        dve.wait_ge(s_at, b)
                    o = w[:].rearrange("p (t h c) -> p t h c", t=LT, h=2 * G)
                    link(V.reciprocal(rd[:, hf], o[:, :, :, DH]))
                    V.tensor_tensor(an[:, :, hf], o[:, :, :, 0:DH],
                                    rd[:, hf][:, :, :, None].to_broadcast([P, LT, 2 * G, DH]), ALU.mult).then_inc(s_an, 1)
                elif kind == "W":
                    dve.wait_ge(s_wo, b + 1)
                    dve.wait_ge(s_xb, b + 1)
                    V.tensor_tensor(x2[:, b], w[:].rearrange("p (t d) -> p t d", t=LT), xb[:, b], ALU.add).then_inc(s_x2, 1)
                    dve.wait_ge(s_x2, b + 1)
                    for t in range(LT):
                        ins = V.bn_stats(stat2[:, t, :], x2[:, b, t, :])
                    link(ins)
                    for t in range(LT):
                        ins = V.bn_aggr(mv2[:, t, :], stat2[:, t, :])
                    ins.then_inc(s_stat2, 1)
                elif kind == "Y":
                    dve.wait_ge(s_rstd2, b + 1)
                    dve.wait_ge(s_stat2, b + 1)
                    for t in range(LT):
                        for k in range(TOPK):
                            ins = V.tensor_scalar(xs[:, LT * b + t, k, 0:D], x2[:, b, t, :], mv2[:, t, 0:1], rstd2[:, t:t + 1],
                                                  ALU.subtract, ALU.mult)
                    ins.then_inc(s_xs, 1)
                elif kind == "G":
                    dve.wait_ge(s_g, b + 1)
                    V.tensor_copy(lg[:], w[:, 0:LT * E].rearrange("p (t e) -> p t e", t=LT)).then_inc(s_lg, 1)
                    dve.wait_ge(s_lg, b + 1)
                    for t in range(LT):
                        ins = V.max(top[:, t, :], lg[:, t, :])
                    link(ins)
                    if b:
                        dve.wait_ge(s_gexp, b)
                    V.tensor_tensor(gap[:], top[:, :, 1], top[:, :, 0], ALU.subtract).then_inc(s_gap, 1)
                    for t in range(LT):
                        ins = V.max_index(topi[:, t, :], top[:, t, :], lg[:, t, :])
                    link(ins)
                    link(V.tensor_copy(topf[:], topi[:, :, 0:TOPK]))
                    for k in range(TOPK):
                        ins = V.tensor_tensor(pick[:, k], topf[:, :, k:k + 1].to_broadcast([P, LT, E]),
                                              lane[:, None, :].to_broadcast([P, LT, E]), ALU.is_equal)
                    link(ins)
                    V.tensor_tensor(chosen[:], pick[:, 0], pick[:, 1], ALU.add).then_inc(s_chosen, 1)
                    dve.wait_ge(s_gexp, b + 1)
                    link(V.tensor_scalar(gden[:], gexp[:], 1.0, None, ALU.add))
                    tb = slice(LT * b, LT * b + LT)
                    link(V.reciprocal(xs[:, tb, 0, D], gden[:]))
                    V.tensor_tensor(xs[:, tb, 1, D], gexp[:], xs[:, tb, 0, D], ALU.mult)
                    V.tensor_copy(xs[:, tb, :, D + 1], ret_row[:, tb, :]).then_inc(s_prob, 1)
                elif kind == "K":
                    tb = slice(LT * b, LT * b + LT)
                    dve.wait_ge(s_rk, b + 1)
                    link(V.tensor_tensor(pos[:], w[:, 0:LT * E].rearrange("p (t e) -> p t e", t=LT),
                                         head[:, None, :].to_broadcast([P, LT, E]), ALU.add))
                    V.tensor_tensor(head[:], head[:], w[:, LT * E:LT * E + E], ALU.add).then_inc(s_pos, 1)
                    for k in range(TOPK):
                        ins = V.tensor_tensor(posk[:, k], pick[:, k], pos[:], ALU.mult)
                    link(ins)
                    for k in range(TOPK):
                        ins = V.tensor_reduce(rowf[:, k], posk[:, k], X, ALU.add)
                    link(ins)
                    V.tensor_copy(row[:, tb, :], rowf[:].rearrange("p k t -> p t k")).then_inc(s_row, 1)

            link(V.tensor_tensor(count[:], head[0:1, :], base[0:1, :], ALU.subtract))
            link(V.tensor_tensor(more[:], count[:, :, None].to_broadcast([1, E, NT]),
                                 steps128[:, None, :].to_broadcast([1, E, NT]), ALU.is_gt))
            link(V.tensor_reduce(ntile[:], more[:], X, ALU.add))
            V.tensor_scalar(skip[:], ntile[:], -1.0, float(SPAN // P), ALU.mult, ALU.add)
            link(V.tensor_tensor_scan(tile_end[:], one8[:], ntile[:], 0.0, ALU.mult, ALU.add))
            link(V.tensor_tensor(ended[:], tile_end[:, None, :].to_broadcast([1, TILES, E]),
                                 tile_no[:, :, None].to_broadcast([1, TILES, E]), ALU.is_le))
            V.tensor_reduce(expf[:], ended[:], X, ALU.add)
            link(V.tensor_tensor(skipped[:], ended[:], skip[:, None, :].to_broadcast([1, TILES, E]), ALU.mult))
            link(V.tensor_reduce(blkf[:], skipped[:], X, ALU.add))
            V.tensor_copy(pad_at[:], head[0:1, :])
            V.tensor_scalar(tile_expert[:], expf[:], float(E - 1), None, ALU.min)
            V.tensor_tensor(tile_block[:], blkf[:], tile_no[:], ALU.add).then_inc(s_tab, 1)

            def step(t, c):
                if 0 <= c <= LAST:
                    dve.wait_ge(s_silu, t + 1)
                    dve.wait_ge(s_up, t + 1)
                    at_least(dve, s_h, t - 1)
                    V.tensor_tensor(hid[:, c % 2, :], st[:, 2 + c % 2, :], sg[:, c % 2, :], ALU.mult).then_inc(s_hid, 1)
                if c + 1 <= LAST:
                    dve.wait_ge(s_ld[(c + 1) % 2], 8 * (t + 1 - (c + 1) % 2) + 16)
                    V.tensor_copy(meta[:, bass.ds(t + 1, 1), :].rearrange("p a w -> p (a w)"), xt[:, (c + 1) % 2, D:D + 2]).then_inc(s_meta, 1)
                if c >= 2:
                    dve.wait_ge(s_d, t - 1)
                    at_least(dve, s_ret[c % 2], 8 * (t - 2 - c % 2))
                    dve.wait_ge(s_meta, t - 1)
                    V.tensor_copy(ridx[:, c % 2:c % 2 + 1], meta[:, bass.ds(t - 2, 1), 1])
                    V.tensor_scalar(ysb[:, c % 2, :], work[1][:, 0:D], meta[:, bass.ds(t - 2, 1), 0], None, ALU.mult).then_inc(s_y, 1)
            pipeline(dve, step)
            for b in range(B):
                dve.wait_ge(s_yb[b], 16)
                for k in range(TOPK):
                    V.tensor_tensor(x2[:, b], x2[:, b], yb[:, LT * b:LT * b + LT, k, :], ALU.add).then_inc(s_fin, 1)
                    dve.wait_ge(s_fin, 2 * b + k + 1)


def _layout(inputs):
    import numpy as np
    f = np.float32
    x = np.ascontiguousarray(inputs["x"])
    c = np.asarray(inputs["ctx_768"])
    ctxT = np.ones((C + 1, B * M), f)
    ctxT[:C] = c.reshape(B * M, C).T
    Wq, bq = np.asarray(inputs["L0_xattn_Wq"]), np.asarray(inputs["L0_xattn_bq"])
    Wkv, bkv = np.asarray(inputs["L0_xattn_Wkv"]), np.asarray(inputs["L0_xattn_bkv"])
    wq = np.zeros((D, QD, P), f); bqs = np.zeros((P, QD), f)
    wk = np.zeros((C + 1, QD, P), f); wv = np.zeros((C + 1, D), f)
    for h in range(H):
        i, g = divmod(h, G)
        for first in (ROW_HI, ROW_LO, ROW_KLO):
            r = 32 * g + first
            wq[:, i, r:r + DH] = Wq[DH * h:DH * h + DH].T
            bqs[r:r + DH, i] = bq[DH * h:DH * h + DH]
            wk[:C, i, r:r + DH] = Wkv[2 * DH * h:2 * DH * h + DH].T
            wk[C, i, r:r + DH] = bkv[2 * DH * h:2 * DH * h + DH]
        wk[C, i, 32 * g + ROW_MAX:32 * g + ROW_MAX + 2] = 1.0
        wv[:C, DH * h:DH * h + DH] = Wkv[2 * DH * h + DH:2 * DH * h + 2 * DH].T
        wv[C, DH * h:DH * h + DH] = bkv[2 * DH * h + DH:2 * DH * h + 2 * DH]
    Wo = np.asarray(inputs["L0_xattn_Wo"])
    wo = np.zeros((D, D), f)
    for hf in range(2):
        for g in range(G):
            for j in range(2):
                h = G * (2 * hf + j) + g
                r = 64 * hf + (2 * g + j) * DH
                wo[r:r + DH] = Wo[:, DH * h:DH * h + DH].T
    bo = np.ascontiguousarray(np.broadcast_to(np.asarray(inputs["L0_xattn_bo"]), (P, D)))
    gateT = np.ascontiguousarray(np.asarray(inputs["L0_ffn_gate_w"]).T)
    wg, wu, wd = (np.asarray(inputs["L0_ffn_" + n]) for n in ("wg", "wu", "wd"))
    wgu = np.ascontiguousarray(np.concatenate([wg.transpose(0, 2, 1), wu.transpose(0, 2, 1)], axis=2))
    wdT = np.ascontiguousarray(wd.transpose(0, 2, 1).reshape(E, IC, P, D).transpose(0, 2, 1, 3).reshape(E, P, IC * D))
    return dict(x=x, ctxT=ctxT, wq=wq, bq=bqs, wk=wk, wv=wv, wo=wo, bo=bo, gateT=gateT, wgu=wgu, wd=wdT)


def kernel(**inputs):
    import concourse.bacc as _bacc
    from concourse.bass_utils import run_bass_kernel_spmd as _run

    nc = _bacc.Bacc("TRN2", target_bir_lowering=False, num_devices=1)
    arrays = _layout(inputs)
    args = {n: nc.dram_tensor(n + "_dram", a.shape, F32, kind="ExternalInput").ap() for n, a in arrays.items()}
    out = nc.dram_tensor("out_dram", (B, L, D), F32, kind="ExternalOutput").ap()
    xattn_moe(nc, out=out, **args)
    r = _run(nc, [{n + "_dram": a for n, a in arrays.items()}], core_ids=[0])
    return r.results[0]["out_dram"]
```

```python
from contextlib import ExitStack

import concourse.bass as bass
from concourse import mybir

ALU = mybir.AluOpType
ACT = mybir.ActivationFunctionType
F32 = mybir.dt.float32
F32R = mybir.dt.float32r
BF16 = mybir.dt.bfloat16
U32 = mybir.dt.uint32
X = mybir.AxisListType.X

P = 128
B, L, D = 4, 512, 128
LT = L // P
NT = B * LT
M, C = 77, 96
H, DH = 16, 8
G = 4
QD = H // G
E, I, TOPK = 8, 512, 2
IC = I // P
EPS = 1e-5
SCALE = float(DH) ** -0.5

ROW_HI, ROW_LO, ROW_KLO, ROW_MAX = 0, 8, 16, 24

SPAN = B * L + P
TILES = B * L * TOPK // P + E - 1
DUMMY = TILES - B * L * TOPK // P
ROWW = D + 2
RET = B * L * TOPK
LAST = TILES - 1
WARM = 24


def xattn_moe(nc, x, ctxT, wq, bq, wk, wv, wo, bo, gateT, wgu, wd, low, out):
    xg = nc.dram_tensor("xg", (E * SPAN + DUMMY * P, ROWW), F32, kind="Internal").ap()
    yr = nc.dram_tensor("yr", (RET + P, D), F32, kind="Internal").ap()

    with ExitStack() as ctx:
        def sb(name, shape, dt=F32):
            return ctx.enter_context(nc.sbuf_tensor(name, shape, dt))

        def sem(name):
            return ctx.enter_context(nc.semaphore(name))

        tok = sb("tok", [P, 3, B, LT, D])
        xa, xn, xb = tok[:, 0], tok[:, 1], tok[:, 2]
        ctxT_s = sb("ctxT_s", [C + 1, B * M])
        wq_s = sb("wq_s", [D, QD, P])
        bq_s = sb("bq_s", [P, QD])
        wk_s = sb("wk_s", [C + 1, QD, P])
        wv_s = sb("wv_s", [C + 1, D])
        wo_s = sb("wo_s", [D, D])
        bo_s = sb("bo_s", [P, D])
        gateT_s = sb("gateT_s", [D, E])
        wgu_s = sb("wgu_s", [D, E, 2 * I])
        wd_s = sb("wd_s", [P, E, IC * D])

        ident = sb("ident", [P, P])
        before = sb("before", [P, P], BF16)
        ones = sb("ones", [P, P], BF16)
        negpow = sb("negpow", [P, LT])
        low_rows = sb("low_rows", [P, 2])
        q_lo, k_lo = low_rows[:, 0:1], low_rows[:, 1:2]
        lane = sb("lane", [P, E])
        ret_row = sb("ret_row", [P, NT, TOPK])

        stat = sb("stat", [P, LT, 6])
        mv1 = sb("mv1", [P, B, LT, 2])
        ve1 = sb("ve1", [P, B, LT])
        rstd1 = sb("rstd1", [P, B, LT])
        xnT = sb("xnT", [D, 2, L])
        qt = sb("qt", [P, 2, L])
        qr = sb("qr", [P, 2, L], F32R)
        qs = sb("qs", [P, 2, QD, L], F32R)
        kr = sb("kr", [P, QD, B * M], F32R)
        ks = sb("ks", [P, QD, B, G, M], F32R)
        vp = sb("vp", [M, B, 2, 2, G, 32])
        nmx = sb("nmx", [P, 2, LT, G, QD])
        nmp = sb("nmp", [P, 2, LT, 2, G * QD], F32R)
        nmT = sb("nmT", [2 * H, 2, L], F32R)
        ER = 4
        ex = sb("ex", [M, ER, 2, L])
        osb = sb("osb", [P, 2, L])
        rd = sb("rd", [P, 2, LT, 2 * G])
        an = sb("an", [P, LT, 2, 2 * G, DH])
        anT = sb("anT", [D, L])
        x2 = sb("x2", [P, B, LT, D])
        stat2 = sb("stat2", [P, LT, 6])
        mv2 = sb("mv2", [P, LT, 2])
        ve2 = sb("ve2", [P, LT])
        rstd2 = sb("rstd2", [P, LT])
        xs = sb("xs", [P, NT, TOPK, ROWW])
        yb = xs[:].rearrange("p t k w -> p (t k w)")[:, 0:NT * TOPK * D].rearrange("p (t k d) -> p t k d", k=TOPK, d=D)
        x2T = sb("x2T", [D, L])
        lg = sb("lg", [P, LT, E])
        top = sb("top", [P, LT, 8])
        topi = sb("topi", [P, LT, 8], U32)
        topf = sb("topf", [P, LT, TOPK])
        pick = sb("pick", [P, TOPK, LT, E])
        chosen = sb("chosen", [P, LT, E], BF16)
        gap = sb("gap", [P, LT])
        gexp = sb("gexp", [P, LT])
        gden = sb("gden", [P, LT])
        head = sb("head", [P, E])
        pos = sb("pos", [P, LT, E])
        posk = sb("posk", [P, TOPK, LT, E])
        rowf = sb("rowf", [P, TOPK, LT])
        row = sb("row", [P, NT, TOPK], U32)

        base = sb("base", [P, E])
        steps128 = sb("steps128", [1, NT])
        tile_no = sb("tile_no", [1, TILES])
        count = sb("count", [1, E])
        more = sb("more", [1, E, NT])
        ntile = sb("ntile", [1, E])
        one8 = sb("one8", [1, E])
        tile_end = sb("tile_end", [1, E])
        ended = sb("ended", [1, TILES, E])
        skip = sb("skip", [1, E])
        skipped = sb("skipped", [1, TILES, E])
        expf = sb("expf", [1, TILES])
        blkf = sb("blkf", [1, TILES])
        tile_expert = sb("tile_expert", [1, TILES], U32)
        tile_block = sb("tile_block", [1, TILES], U32)
        pad_at = sb("pad_at", [1, E], U32)
        padrow = sb("padrow", [P, ROWW])
        warm = sb("warm", [P, 1])
        xt = tok[:, 0].rearrange("p b t d -> p (b t d)")[:, 0:2 * ROWW].rearrange("p (n w) -> p n w", n=2)
        eT = tok[:, 1, 0, 0:2]
        ysb = tok[:, 2, 0, 0:2]
        meta = sb("meta", [P, TILES, 2])
        sg, hid, hT = qt, osb, xnT
        ridx = sb("ridx", [P, 2], U32)

        work = [ctx.enter_context(nc.psum_tensor(f"work{n}", [P, 512], F32)) for n in range(3)]
        opv = ctx.enter_context(nc.psum_tensor("opv", [P, 512], F32))
        st = ctx.enter_context(nc.psum_tensor("st", [P, G, 512], F32))
        hT_bank = [opv, work[2]]

        s_x = [sem(f"s_xin{b}") for b in range(B)]
        s_wk = sem("s_wk"); s_wq = sem("s_wq"); s_wvo = sem("s_wvo"); s_moew = sem("s_moew")
        s_id = sem("s_id"); s_cst = sem("s_cst"); s_pool = sem("s_pool")
        s_dve = sem("s_dve")
        s_stat1 = sem("s_stat1"); s_rstd1 = sem("s_rstd1"); s_xn = sem("s_xn"); s_xb = sem("s_xb")
        s_kps = sem("s_kps"); s_kr = sem("s_kr"); s_ksr = sem("s_ksr"); s_kz = sem("s_kz")
        s_ks = sem("s_ks"); s_ks2 = sem("s_ks2")
        s_vps = sem("s_vps"); s_vp = sem("s_vp")
        s_xT = sem("s_xT"); s_xnT = sem("s_xnT")
        s_q = sem("s_q"); s_qt = sem("s_qt"); s_qs = sem("s_qs")
        s_l = sem("s_l"); s_mx = sem("s_mx"); s_nt = sem("s_nt"); s_nmp = sem("s_nmp"); s_nm = sem("s_nm")
        s_nmd = [sem(f"s_nmd{n}") for n in range(2)]
        s_s = sem("s_s"); s_e = sem("s_e"); s_pv = sem("s_pv"); s_osb = sem("s_osb")
        s_ot = sem("s_ot"); s_an = sem("s_an"); s_at = sem("s_at"); s_anT = sem("s_anT")
        s_wo = sem("s_wo"); s_x2 = sem("s_x2"); s_stat2 = sem("s_stat2"); s_rstd2 = sem("s_rstd2")
        s_xs = sem("s_xs"); s_xs1 = sem("s_xs1"); s_x2t = sem("s_x2t"); s_x2T = sem("s_x2T")
        s_g = sem("s_g"); s_lg = sem("s_lg"); s_gap = sem("s_gap"); s_gexp = sem("s_gexp"); s_prob = sem("s_prob")
        s_chosen = sem("s_chosen"); s_rk = sem("s_rk"); s_pos = sem("s_pos"); s_row = sem("s_row")
        s_disp = sem("s_disp"); s_out = sem("s_out")
        s_warm = sem("s_warm"); s_pad = sem("s_pad"); s_padw = sem("s_padw"); s_tab = sem("s_tab")
        s_ld = [sem(f"s_ld{n}") for n in range(2)]
        s_meta = sem("s_meta")
        s_t = sem("s_t"); s_eT = sem("s_eT"); s_gate = sem("s_gate"); s_up = sem("s_up")
        s_silu = sem("s_silu"); s_hid = sem("s_hid"); s_h = sem("s_h"); s_hT = sem("s_hT")
        s_d = sem("s_d"); s_y = sem("s_y")
        s_ret = [sem(f"s_ret{n}") for n in range(2)]
        s_yb = [sem(f"s_yb{n}") for n in range(B)]
        s_fin = sem("s_fin")

        PAIRS, EARLY = H // 2, 3

        def to_scores(b):
            return ([("X", b)] + [("Q", b, i) for i in range(QD)] +
                    [("R", b, lt, i) for lt in range(LT) for i in range(QD)] + [("T", b)])

        def from_values(b):
            return [[("O", b, 0)], [("O", b, 1)], [("A", b)], [("W", b)], [], [("Y", b)], [("G", b)], [("K", b)]]

        steps = [("M", 0), ("KP", 0), ("N", 0), ("KP", 1), ("KB", 0), ("KP", 2), ("KB", 1), ("KP", 3), ("KB", 2)]
        first = to_scores(0)
        steps += first[:2] + [("KB", 3)] + first[2:9] + [("M", 1)] + first[9:13] + [("N", 1)] + first[13:] + [("VP", 0)]
        queue = []
        for n in range(B * PAIRS + 1):
            b, j = divmod(n, PAIRS)
            if n < B * PAIRS:
                steps.append(("S", b, j))
            if n == 0 or (n + EARLY) % PAIRS == 0:
                nxt = (n + EARLY) // PAIRS + 1
                if nxt < B:
                    queue += to_scores(nxt)
            steps += queue[:3]
            queue = queue[3:]
            if n:
                steps.append(("V", (n - 1) // PAIRS, (n - 1) % PAIRS))
            if n < 2 * PAIRS and n % PAIRS == 1:
                steps.append(("M", n // PAIRS + 2))
            if n < 2 * PAIRS and n % PAIRS == 3:
                steps.append(("N", n // PAIRS + 2))
            if b and n < B * PAIRS:
                steps += from_values(b - 1)[j]
        steps += sum(from_values(B - 1), [])

        reader = {"X": (s_xnT, lambda b: b + 1), "Q": (s_qt, lambda b, i: QD * b + i + 1),
                  "R": (s_mx, lambda b, lt, i: NT * b + QD * lt + i + 1), "T": (s_nm, lambda b: b + 1),
                  "O": (s_an, lambda b, h: 2 * b + h + 1), "A": (s_anT, lambda b: b + 1),
                  "W": (s_x2, lambda b: b + 1), "Y": (s_x2T, lambda b: b + 1),
                  "G": (s_lg, lambda b: b + 1), "K": (s_pos, lambda b: b + 1)}
        uses = [s for s in steps if s[0] in reader]
        turn = {s: n for n, s in enumerate(uses)}

        def claim(eng, s):
            n = turn[s]
            if n >= 3:
                who, value = reader[uses[n - 3][0]]
                eng.wait_ge(who, value(*uses[n - 3][1:]))
            return work[n % 3]

        FIRST, STOP = 4, LAST
        assert (STOP - FIRST) % 2 == 0

        def pipeline(eng, step):
            for t in range(-1, FIRST):
                step(t, t)
            with eng.Fori(0, (STOP - FIRST) // 2) as i:
                for c in range(2):
                    step(2 * i + FIRST + c, FIRST + c)
            for t in range(STOP, LAST + 3):
                step(t, t)

        def at_least(eng, s, value):
            if not isinstance(value, int) or value > 0:
                eng.wait_ge(s, value)

        block = ctx.enter_context(nc.Block())

        @block.sync
        def _(sp):
            def load_x(b):
                sp.dma_start(xa[:, b], x[b].rearrange("(t p) d -> p t d", p=P)).then_inc(s_x[b], 16)

            load_x(0)
            for dst, src in ((ctxT_s, ctxT), (wk_s, wk), (low_rows, low)):
                sp.dma_start(dst[:], src).then_inc(s_wk, 16)
            for dst, src in ((wq_s, wq), (bq_s, bq)):
                sp.dma_start(dst[:], src).then_inc(s_wq, 16)
            for b in range(1, B):
                load_x(b)
            for dst, src in ((wv_s, wv), (wo_s, wo), (bo_s, bo), (gateT_s, gateT)):
                sp.dma_start(dst[:], src).then_inc(s_wvo, 16)
            for e in range(E):
                sp.dma_start(wgu_s[:, e, :], wgu[e]).then_inc(s_moew, 16)
                sp.dma_start(wd_s[:, e, :], wd[e]).then_inc(s_moew, 16)
            sp.wait_ge(s_pad, 1)
            sp.dma_start(xg[E * SPAN:E * SPAN + P * DUMMY, :].rearrange("(n p) w -> p n w", p=P),
                         padrow[:, None, :].to_broadcast([P, DUMMY, ROWW])).then_inc(s_padw, 16)
            for b in range(B):
                sp.wait_ge(s_nm, b + 1)
                for n in range(2):
                    sp.dma_start(qs[ROW_MAX + n:P:32, b % 2, :, :].bitcast(F32),
                                 nmT[H * n:H * n + H, b % 2, :].bitcast(F32)).then_inc(s_nmd[b % 2], 16)
            sp.wait_ge(s_tab, 1)
            for e in range(0, E, 2):
                at = sp.value_load(pad_at[0:1, e:e + 1], min_val=e * SPAN, max_val=e * SPAN + B * L)
                sp.dma_start(xg[bass.ds(at, P), :], padrow[:]).then_inc(s_padw, 16)
            sp.wait_ge(s_padw, 16 * (E + 1))
            sp.wait_ge(s_disp, 16 * NT * TOPK)
            blocks = xg.rearrange("(n p) w -> n p w", p=P)

            def load(t, c):
                blk = sp.value_load(tile_block[0:1, bass.ds(t, 1)], min_val=0, max_val=E * SPAN // P + DUMMY - 1)
                at_least(sp, s_t, t - 1)
                at_least(sp, s_meta, t - 1)
                sp.dma_start(xt[:, c % 2, :],
                             blocks[bass.ds(blk, 1)].rearrange("a p w -> (a p) w")).then_inc(s_ld[c % 2], 16)

            load(0, 0)
            load(1, 1)
            with sp.Fori(1, (TILES - 1) // 2) as i:
                for c in range(2):
                    load(2 * i + c, 2 + c)
            load(LAST, LAST)
            for n in range(2):
                sp.wait_ge(s_ret[n], 16 * ((TILES + 1 - n) // 2))
            for b in range(B):
                sp.dma_start(yb[:, LT * b:LT * b + LT].rearrange("p t k d -> p t (k d)"),
                             yr[TOPK * L * b:TOPK * L * (b + 1), :].rearrange("(t p k) d -> p t (k d)", p=P, k=TOPK)).then_inc(s_yb[b], 16)
            for b in range(B):
                sp.wait_ge(s_fin, 2 * b + 2)
                sp.dma_start(out[b].rearrange("(t p) d -> p t d", p=P), x2[:, b]).then_inc(s_out, 16)
            sp.wait_ge(s_out, 16 * B)

        @block.gpsimd
        def _(pool):
            pool.memset(ident[:], 0.0).then_inc(s_pool, 1)
            pool.memset(before[:], 1.0).then_inc(s_pool, 1)
            pool.wait_ge(s_pool, 1)
            pool.affine_select(out=ident[:], in_=ident[:], compare_op=ALU.not_equal, fill=1.0, base=0,
                               pattern=[[-1, P]], channel_multiplier=1).then_inc(s_id, 1)
            pool.memset(negpow[:], -0.5).then_inc(s_pool, 1)
            pool.memset(vp[:], 0.0).then_inc(s_pool, 1)
            done = 4

            def rstd_1(b):
                nonlocal done
                pool.wait_ge(s_stat1, b + 1)
                pool.tensor_scalar(ve1[:, b], mv1[:, b, :, 1], EPS, None, ALU.add).then_inc(s_pool, 1)
                done += 1
                pool.wait_ge(s_pool, done)
                pool.tensor_tensor(rstd1[:, b], ve1[:, b], negpow[:], ALU.pow).then_inc(s_rstd1, 1)

            rstd_1(0)
            for j in range(2):
                pool.memset(vp[:, :, :, j, :, 16 * j + DH:16 * j + DH + 1], 1.0).then_inc(s_cst, 1)
            pool.affine_select(out=before[:], in_=before[:], compare_op=ALU.is_gt, fill=0.0, base=0,
                               pattern=[[1, P]], channel_multiplier=-1).then_inc(s_cst, 1)
            pool.memset(ones[:], 1.0).then_inc(s_cst, 1)
            pool.iota(lane[:], [[1, E]], base=0, channel_multiplier=0,
                      allow_small_or_imprecise_dtypes=True).then_inc(s_cst, 1)
            pool.iota(head[:], [[SPAN, E]], base=0, channel_multiplier=0,
                      allow_small_or_imprecise_dtypes=True).then_inc(s_cst, 1)
            pool.iota(ret_row[:], [[TOPK * P, NT], [1, TOPK]], base=0, channel_multiplier=TOPK,
                      allow_small_or_imprecise_dtypes=True).then_inc(s_cst, 1)
            rstd_1(1)
            pool.memset(padrow[:], 0.0).then_inc(s_pool, 1)
            done += 1
            pool.wait_ge(s_pool, done)
            pool.iota(padrow[:, D + 1:D + 2], [[0, 1]], base=RET, channel_multiplier=1,
                      allow_small_or_imprecise_dtypes=True).then_inc(s_pad, 1)
            pool.iota(base[:], [[SPAN, E]], base=0, channel_multiplier=0,
                      allow_small_or_imprecise_dtypes=True).then_inc(s_cst, 1)
            pool.iota(steps128[:], [[P, NT]], base=0, channel_multiplier=0,
                      allow_small_or_imprecise_dtypes=True).then_inc(s_cst, 1)
            pool.iota(tile_no[:], [[1, TILES]], base=0, channel_multiplier=0,
                      allow_small_or_imprecise_dtypes=True).then_inc(s_cst, 1)
            pool.memset(one8[:], 1.0).then_inc(s_cst, 1)
            pool.wait_ge(s_wvo, 16 * 4)
            for b in range(B):
                if b >= 2:
                    rstd_1(b)
                pool.wait_ge(s_x[b], 16)
                pool.tensor_tensor(xb[:, b], xa[:, b], bo_s[:, None, :].to_broadcast([P, LT, D]), ALU.add).then_inc(s_xb, 1)
            for b in range(B):
                pool.wait_ge(s_stat2, b + 1)
                pool.tensor_scalar(ve2[:], mv2[:, :, 1], EPS, None, ALU.add).then_inc(s_pool, 1)
                done += 1
                pool.wait_ge(s_pool, done)
                if b:
                    pool.wait_ge(s_xs, b)
                pool.tensor_tensor(rstd2[:], ve2[:], negpow[:], ALU.pow).then_inc(s_rstd2, 1)
                pool.wait_ge(s_xs, b + 1)
                pool.tensor_copy(xs[:, LT * b:LT * b + LT, 1, 0:D], xs[:, LT * b:LT * b + LT, 0, 0:D]).then_inc(s_pool, 1)
                done += 1
                pool.wait_ge(s_pool, done)
                pool.wait_ge(s_prob, b + 1)
                pool.wait_ge(s_row, b + 1)
                for t in range(LT * b, LT * b + LT):
                    for k in range(TOPK):
                        pool.indirect_dma_start(out=xg, out_offset=bass.IndirectOffsetOnAxis(ap=row[:, t, k:k + 1], axis=0),
                                                in_=xs[:, t, k, :], in_offset=None).then_inc(s_disp, 16)

            last_row = pool.to_reg(RET - 1)
            def step(t, c):
                if c >= 2:
                    pool.wait_ge(s_y, t - 1)
                    pool.nop(nofuse=True)
                    pool.indirect_dma_start(out=yr, out_offset=bass.IndirectOffsetOnAxis(ap=ridx[:, c % 2:c % 2 + 1], axis=0),
                                            in_=ysb[:, c % 2, :], in_offset=None,
                                            bounds_check=last_row, oob_is_err=False).then_inc(s_ret[c % 2], 16)
            pipeline(pool, step)

        @block.tensor
        def _(pe):
            pe.wait_ge(s_id, 1)
            for n in range(WARM):
                nc.tensor.transpose(work[0][:, 0:P], ident[:], ident[:])
            for s in steps:
                kind = s[0]
                b = s[1]
                if kind in reader:
                    w = claim(pe, s)
                if kind == "KP":
                    i = s[1]
                    pe.wait_ge(s_wk, 16 * 3)
                    nc.tensor.matmul(st[:, i, 0:B * M], wk_s[:, i, :], ctxT_s[:], start=True, stop=True).then_inc(s_kps, 1)
                elif kind == "VP":
                    pe.wait_ge(s_wvo, 16 * 4)
                    for n in range(B):
                        last = nc.tensor.matmul(opv[0:M, D * n:D * n + D], ctxT_s[:, M * n:M * n + M], wv_s[:], start=True, stop=True)
                    last.then_inc(s_vps, 1)
                elif kind == "X":
                    pe.wait_ge(s_xn, b + 1)
                    for t in range(LT):
                        last = nc.tensor.transpose(w[:, P * t:P * t + P], xn[:, b, t, :], ident[:])
                    last.then_inc(s_xT, 1)
                elif kind == "Q":
                    i = s[2]
                    pe.wait_ge(s_xnT, b + 1)
                    pe.wait_ge(s_wq, 16 * 2)
                    nc.tensor.matmul(w[:], wq_s[:, i, :], xnT[:, b % 2, :], start=True, stop=True).then_inc(s_q, 1)
                elif kind == "R":
                    lt, i = s[2], s[3]
                    pe.wait_ge(s_qs, QD * b + i + 1)
                    if b == 0:
                        pe.wait_ge(s_ks, 2 * (i + 1))
                        pe.wait_ge(s_ks2, 2 * (i + 1))
                    nc.tensor.matmul(w[:, 0:G * M], qs[:, b % 2, i, P * lt:P * lt + P],
                                     ks[:, i, b].rearrange("p g m -> p (g m)"), start=True, stop=True).then_inc(s_l, 1)
                elif kind == "T":
                    pe.wait_ge(s_nmp, b + 1)
                    for t in range(LT):
                        last = nc.tensor.transpose(w[0:2 * H, P * t:P * t + P],
                                                   nmp[:, b % 2, t].bitcast(F32).rearrange("p a h -> p (a h)"), ident[:])
                    last.then_inc(s_nt, 1)
                elif kind == "S":
                    n = PAIRS * b + s[2]
                    i = s[2] // 2
                    pe.wait_ge(s_nmd[b % 2], 32 * (b // 2 + 1))
                    if n >= 2:
                        pe.wait_ge(s_e, n - 1)
                    for g in range(2 * (n % 2), 2 * (n % 2) + 2):
                        last = nc.tensor.matmul(st[0:M, g, :], ks[:, i, b, g, :], qs[:, b % 2, i, :], start=True, stop=True)
                    last.then_inc(s_s, 1)
                elif kind == "V":
                    n = PAIRS * b + s[2]
                    i = s[2] // 2
                    pe.wait_ge(s_vp, 1)
                    if s[2] % (PAIRS // 2) == 0 and n:
                        pe.wait_ge(s_osb, n // (PAIRS // 2))
                    pe.wait_ge(s_e, n + 1)
                    for g in range(2 * (n % 2), 2 * (n % 2) + 2):
                        last = nc.tensor.matmul(opv[32 * g:32 * g + 32, :], vp[:, b, i // 2, i % 2, g, :],
                                                ex[:, n % ER, g % 2, :], start=(i % 2 == 0), stop=(i % 2 == 1),
                                                tile_position=(0, 32 * g))
                    last.then_inc(s_pv, 1)
                elif kind == "O":
                    hf = s[2]
                    pe.wait_ge(s_osb, 2 * b + hf + 1)
                    for t in range(LT):
                        last = nc.tensor.transpose(w[:, P * t:P * t + P], osb[:, hf, P * t:P * t + P], ident[:])
                    last.then_inc(s_ot, 1)
                elif kind == "A":
                    pe.wait_ge(s_an, 2 * (b + 1))
                    for t in range(LT):
                        last = nc.tensor.transpose(w[:, P * t:P * t + P],
                                                   an[:, t].rearrange("p a b d -> p (a b d)"), ident[:])
                    last.then_inc(s_at, 1)
                elif kind == "W":
                    pe.wait_ge(s_anT, b + 1)
                    for t in range(LT):
                        last = nc.tensor.matmul(w[:, P * t:P * t + P], anT[:, P * t:P * t + P], wo_s[:], start=True, stop=True)
                    last.then_inc(s_wo, 1)
                elif kind == "Y":
                    pe.wait_ge(s_xs, b + 1)
                    for t in range(LT):
                        last = nc.tensor.transpose(w[:, P * t:P * t + P], xs[:, LT * b + t, 0, 0:D], ident[:])
                    last.then_inc(s_x2t, 1)
                elif kind == "G":
                    pe.wait_ge(s_x2T, b + 1)
                    for t in range(LT):
                        last = nc.tensor.matmul(w[:, E * t:E * t + E], x2T[:, P * t:P * t + P], gateT_s[:], start=True, stop=True)
                    last.then_inc(s_g, 1)
                elif kind == "K":
                    pe.wait_ge(s_chosen, b + 1)
                    pe.wait_ge(s_cst, 11)
                    nc.tensor.matmul(w[:, 0:LT * E], before[:], chosen[:].rearrange("p t e -> p (t e)"), start=True, stop=False)
                    for t in range(LT - 1):
                        nc.tensor.matmul(w[:, E * (t + 1):LT * E], ones[:],
                                         chosen[:, t:t + 1, :].to_broadcast([P, LT - 1 - t, E]),
                                         start=False, stop=(t == LT - 2))
                    for t in range(LT):
                        last = nc.tensor.matmul(w[:, LT * E:LT * E + E], ones[:], chosen[:, t, :],
                                                start=(t == 0), stop=(t == LT - 1))
                    last.then_inc(s_rk, 1)

            pe.wait_ge(s_e, PAIRS * B)
            pe.wait_ge(s_osb, 2 * B)
            pe.wait_ge(s_pos, B)
            pe.wait_ge(s_moew, 16 * 2 * E)
            pe.wait_ge(s_tab, 1)

            def step(t, c):
                if 0 <= c <= LAST:
                    e = pe.value_load(tile_expert[0:1, bass.ds(t, 1)], min_val=0, max_val=E - 1)
                    pe.wait_ge(s_eT, t + 1)
                    at_least(pe, s_silu, t - 1)
                    at_least(pe, s_hid, t - 1)
                    for n, done in ((0, s_gate), (1, s_up)):
                        nc.tensor.matmul(st[:, 2 * n + c % 2, :], eT[:, c % 2, :],
                                         wgu_s[:, bass.ds(e, 1), I * n:I * n + I].rearrange("p a n -> p (a n)"),
                                         start=True, stop=True).then_inc(done, 1)
                if c + 1 <= LAST:
                    pe.wait_ge(s_ld[(c + 1) % 2], 8 * (t + 1 - (c + 1) % 2) + 16)
                    at_least(pe, s_eT, t + 1)
                    nc.tensor.transpose(work[0][:, 0:P], xt[:, (c + 1) % 2, 0:D], ident[:]).then_inc(s_t, 1)
                if 1 <= c <= LAST + 1:
                    pe.wait_ge(s_hid, t)
                    at_least(pe, s_hT, t - 2)
                    for n in range(IC):
                        last = nc.tensor.transpose(hT_bank[(c + 1) % 2][:, P * n:P * n + P], hid[:, (c + 1) % 2, P * n:P * n + P], ident[:])
                    last.then_inc(s_h, 1)
                if c >= 2:
                    e = pe.value_load(tile_expert[0:1, bass.ds(t - 2, 1)], min_val=0, max_val=E - 1)
                    pe.wait_ge(s_hT, t - 1)
                    at_least(pe, s_y, t - 2)
                    for n in range(IC):
                        last = nc.tensor.matmul(work[1][:, 0:D], hT[:, c % 2, P * n:P * n + P],
                                                wd_s[:, bass.ds(e, 1), D * n:D * n + D].rearrange("p a n -> p (a n)"),
                                                start=(n == 0), stop=(n == IC - 1))
                    last.then_inc(s_d, 1)
            pipeline(pe, step)

        @block.scalar
        def _(act):
            for s in steps:
                kind = s[0]
                b = s[1]
                w = work[turn[s] % 3] if s in turn else None
                if kind == "KP":
                    i = s[1]
                    act.wait_ge(s_kps, i + 1)
                    nc.scalar.copy(kr[:, i, :], st[:, i, 0:B * M]).then_inc(s_kr, 1)
                elif kind == "KB":
                    i = s[1]
                    act.wait_ge(s_kz, i + 1)
                    act.wait_ge(s_ksr, i + 1)
                    for g in range(2, G):
                        r = slice(32 * g, 32 * g + 32)
                        nc.scalar.copy(ks[r, i, :, g, :], kr[r, i, :].bitcast(F32).rearrange("p (b m) -> p b m", b=B)).then_inc(s_ks2, 1)
                elif kind == "VP":
                    act.wait_ge(s_vps, 1)
                    act.wait_ge(s_cst, 2)
                    for hf in range(2):
                        for j in range(2):
                            last = nc.scalar.copy(vp[:, :, hf, j, :, 16 * j:16 * j + DH],
                                                  opv[0:M, :].rearrange("m (b q g d) -> m b q g d", b=B, q=QD, g=G)[:, :, 2 * hf + j])
                    last.then_inc(s_vp, 1)
                elif kind == "X":
                    act.wait_ge(s_xT, b + 1)
                    if b >= 2:
                        act.wait_ge(s_q, QD * (b - 1))
                    nc.scalar.copy(xnT[:, b % 2, :], w[:]).then_inc(s_xnT, 1)
                elif kind == "T":
                    act.wait_ge(s_nt, b + 1)
                    if b >= 2:
                        act.wait_ge(s_nmd[b % 2], 32 * (b // 2))
                    nc.scalar.copy(nmT[:, b % 2, :], w[0:2 * H, :]).then_inc(s_nm, 1)
                elif kind == "Q":
                    i = s[2]
                    n = QD * b + i
                    act.wait_ge(s_q, n + 1)
                    if n >= 2:
                        act.wait_ge(s_qs, n - 1)
                    nc.scalar.activation(qr[:, n % 2, :], w[:], ACT.Identity, bias=bq_s[:, i:i + 1])
                    nc.scalar.activation(qt[:, n % 2, :], w[:], ACT.Identity, bias=bq_s[:, i:i + 1]).then_inc(s_qt, 1)
                elif kind == "S":
                    n = PAIRS * b + s[2]
                    act.wait_ge(s_s, n + 1)
                    if n >= ER:
                        act.wait_ge(s_pv, n - ER + 1)
                    nc.scalar.activation(ex[:, n % ER], st[0:M, 2 * (n % 2):2 * (n % 2) + 2, :], ACT.Exp, scale=SCALE).then_inc(s_e, 1)
                elif kind == "V" and s[2] % (PAIRS // 2) == PAIRS // 2 - 1:
                    hf = s[2] // (PAIRS // 2)
                    act.wait_ge(s_pv, PAIRS * b + s[2] + 1)
                    if b:
                        act.wait_ge(s_ot, 2 * (b - 1) + hf + 1)
                    nc.scalar.copy(osb[:, hf, :], opv[:]).then_inc(s_osb, 1)
                elif kind == "A":
                    act.wait_ge(s_at, b + 1)
                    if b:
                        act.wait_ge(s_wo, b)
                    nc.scalar.copy(anT[:], w[:]).then_inc(s_anT, 1)
                elif kind == "Y":
                    act.wait_ge(s_x2t, b + 1)
                    if b:
                        act.wait_ge(s_g, b)
                    nc.scalar.copy(x2T[:], w[:]).then_inc(s_x2T, 1)
                elif kind == "G":
                    act.wait_ge(s_gap, b + 1)
                    nc.scalar.activation(gexp[:], gap[:], ACT.Exp).then_inc(s_gexp, 1)

            act.wait_ge(s_pad, 1)
            nc.scalar.activation(warm[:], padrow[:, 0:1], ACT.Silu).then_inc(s_warm, 1)
            act.wait_ge(s_tab, 1)
            for e in range(1, E, 2):
                at = act.value_load(pad_at[0:1, e:e + 1], min_val=e * SPAN, max_val=e * SPAN + B * L)
                act.dma_start(xg[bass.ds(at, P), :], padrow[:]).then_inc(s_padw, 16)

            def step(t, c):
                if 0 <= c <= LAST:
                    act.wait_ge(s_gate, t + 1)
                    at_least(act, s_hid, t - 1)
                    nc.scalar.activation(sg[:, c % 2, :], st[:, c % 2, :], ACT.Silu).then_inc(s_silu, 1)
                if c + 1 <= LAST:
                    act.wait_ge(s_t, t + 2)
                    at_least(act, s_up, t)
                    nc.scalar.copy(eT[:, (c + 1) % 2, :], work[0][:, 0:P]).then_inc(s_eT, 1)
                if 1 <= c <= LAST + 1:
                    act.wait_ge(s_h, t)
                    at_least(act, s_d, t - 2)
                    nc.scalar.copy(hT[:, (c + 1) % 2, :], hT_bank[(c + 1) % 2][:]).then_inc(s_hT, 1)
            pipeline(act, step)

        @block.vector
        def _(dve):
            chain = [0]

            def link(ins):
                chain[0] += 1
                ins.then_inc(s_dve, 1)
                dve.wait_ge(s_dve, chain[0])

            V = nc.vector

            def stats1(b):
                dve.wait_ge(s_x[b], 16)
                for t in range(LT):
                    ins = V.bn_stats(stat[:, t, :], xa[:, b, t, :])
                link(ins)
                for t in range(LT):
                    ins = V.bn_aggr(mv1[:, b, t, :], stat[:, t, :])
                ins.then_inc(s_stat1, 1)

            def norm1(b):
                dve.wait_ge(s_stat1, b + 1)
                dve.wait_ge(s_rstd1, b + 1)
                for t in range(LT):
                    ins = V.tensor_scalar(xn[:, b, t, :], xa[:, b, t, :], mv1[:, b, t, 0:1], rstd1[:, b, t:t + 1],
                                          ALU.subtract, ALU.mult)
                ins.then_inc(s_xn, 1)

            for i in range(QD):
                V.memset(ks[:, i].rearrange("p b c d -> p (b c d)").bitcast(F32), 0.0).then_inc(s_kz, 1)
            for s in steps:
                kind = s[0]
                b = s[1]
                w = work[turn[s] % 3] if s in turn else None
                if kind == "M":
                    stats1(b)
                elif kind == "N":
                    norm1(b)
                elif kind == "KP":
                    i = s[1]
                    dve.wait_ge(s_kr, i + 1)
                    dve.wait_ge(s_wk, 16 * 3)
                    V.scalar_tensor_tensor(kr[:, i, :], kr[:, i, :].bitcast(F32), k_lo, st[:, i, 0:B * M],
                                           ALU.mult, ALU.add).then_inc(s_ksr, 1)
                elif kind == "KB":
                    i = s[1]
                    dve.wait_ge(s_kz, i + 1)
                    dve.wait_ge(s_ksr, i + 1)
                    for g in range(2):
                        r = slice(32 * g, 32 * g + 32)
                        V.tensor_copy(ks[r, i, :, g, :], kr[r, i, :].bitcast(F32).rearrange("p (b m) -> p b m", b=B)).then_inc(s_ks, 1)
                elif kind == "Q":
                    n = QD * b + s[2]
                    dve.wait_ge(s_qt, n + 1)
                    if b >= 2:
                        dve.wait_ge(s_s, PAIRS * (b - 2) + 2 * s[2] + 2)
                    V.scalar_tensor_tensor(qs[:, b % 2, s[2], :], qr[:, n % 2, :].bitcast(F32), q_lo,
                                           qt[:, n % 2, :], ALU.mult, ALU.add).then_inc(s_qs, 1)
                elif kind == "R":
                    lt, i = s[2], s[3]
                    n = NT * b + QD * lt + i
                    dve.wait_ge(s_l, n + 1)
                    V.tensor_reduce(nmx[:, b % 2, lt, :, i], w[:, 0:G * M].rearrange("p (g m) -> p g m", g=G),
                                    X, ALU.max, negate=True).then_inc(s_mx, 1)
                elif kind == "T":
                    m = nmx[:, b % 2].rearrange("p t g i -> p t (g i)")
                    dve.wait_ge(s_mx, NT * (b + 1))
                    link(V.tensor_copy(nmp[:, b % 2, :, 0], m))
                    V.tensor_tensor(nmp[:, b % 2, :, 1], m, nmp[:, b % 2, :, 0].bitcast(F32), ALU.subtract).then_inc(s_nmp, 1)
                elif kind == "O":
                    hf = s[2]
                    dve.wait_ge(s_ot, 2 * b + hf + 1)
                    if b and hf == 0:
                        dve.wait_ge(s_at, b)
                    o = w[:].rearrange("p (t h c) -> p t h c", t=LT, h=2 * G)
                    link(V.reciprocal(rd[:, hf], o[:, :, :, DH]))
                    V.tensor_tensor(an[:, :, hf], o[:, :, :, 0:DH],
                                    rd[:, hf][:, :, :, None].to_broadcast([P, LT, 2 * G, DH]), ALU.mult).then_inc(s_an, 1)
                elif kind == "W":
                    dve.wait_ge(s_wo, b + 1)
                    dve.wait_ge(s_xb, b + 1)
                    V.tensor_tensor(x2[:, b], w[:].rearrange("p (t d) -> p t d", t=LT), xb[:, b], ALU.add).then_inc(s_x2, 1)
                    dve.wait_ge(s_x2, b + 1)
                    for t in range(LT):
                        ins = V.bn_stats(stat2[:, t, :], x2[:, b, t, :])
                    link(ins)
                    for t in range(LT):
                        ins = V.bn_aggr(mv2[:, t, :], stat2[:, t, :])
                    ins.then_inc(s_stat2, 1)
                elif kind == "Y":
                    dve.wait_ge(s_rstd2, b + 1)
                    dve.wait_ge(s_stat2, b + 1)
                    for t in range(LT):
                        ins = V.tensor_scalar(xs[:, LT * b + t, 0, 0:D], x2[:, b, t, :], mv2[:, t, 0:1], rstd2[:, t:t + 1],
                                              ALU.subtract, ALU.mult)
                    ins.then_inc(s_xs, 1)
                elif kind == "G":
                    dve.wait_ge(s_g, b + 1)
                    if b == 0:
                        dve.wait_ge(s_cst, 11)
                    V.tensor_copy(lg[:], w[:, 0:LT * E].rearrange("p (t e) -> p t e", t=LT)).then_inc(s_lg, 1)
                    dve.wait_ge(s_lg, b + 1)
                    for t in range(LT):
                        ins = V.max(top[:, t, :], lg[:, t, :])
                    link(ins)
                    if b:
                        dve.wait_ge(s_gexp, b)
                    V.tensor_tensor(gap[:], top[:, :, 1], top[:, :, 0], ALU.subtract).then_inc(s_gap, 1)
                    for t in range(LT):
                        ins = V.max_index(topi[:, t, :], top[:, t, :], lg[:, t, :])
                    link(ins)
                    link(V.tensor_copy(topf[:], topi[:, :, 0:TOPK]))
                    for k in range(TOPK):
                        ins = V.tensor_tensor(pick[:, k], topf[:, :, k:k + 1].to_broadcast([P, LT, E]),
                                              lane[:, None, :].to_broadcast([P, LT, E]), ALU.is_equal)
                    link(ins)
                    V.tensor_tensor(chosen[:], pick[:, 0], pick[:, 1], ALU.add).then_inc(s_chosen, 1)
                    dve.wait_ge(s_gexp, b + 1)
                    link(V.tensor_scalar(gden[:], gexp[:], 1.0, None, ALU.add))
                    tb = slice(LT * b, LT * b + LT)
                    link(V.reciprocal(xs[:, tb, 0, D], gden[:]))
                    V.tensor_tensor(xs[:, tb, 1, D], gexp[:], xs[:, tb, 0, D], ALU.mult)
                    V.tensor_copy(xs[:, tb, :, D + 1], ret_row[:, tb, :]).then_inc(s_prob, 1)
                elif kind == "K":
                    tb = slice(LT * b, LT * b + LT)
                    dve.wait_ge(s_rk, b + 1)
                    link(V.tensor_tensor(pos[:], w[:, 0:LT * E].rearrange("p (t e) -> p t e", t=LT),
                                         head[:, None, :].to_broadcast([P, LT, E]), ALU.add))
                    V.tensor_tensor(head[:], head[:], w[:, LT * E:LT * E + E], ALU.add).then_inc(s_pos, 1)
                    for k in range(TOPK):
                        ins = V.tensor_tensor(posk[:, k], pick[:, k], pos[:], ALU.mult)
                    link(ins)
                    for k in range(TOPK):
                        ins = V.tensor_reduce(rowf[:, k], posk[:, k], X, ALU.add)
                    link(ins)
                    V.tensor_copy(row[:, tb, :], rowf[:].rearrange("p k t -> p t k")).then_inc(s_row, 1)

            link(V.tensor_tensor(count[:], head[0:1, :], base[0:1, :], ALU.subtract))
            link(V.tensor_tensor(more[:], count[:, :, None].to_broadcast([1, E, NT]),
                                 steps128[:, None, :].to_broadcast([1, E, NT]), ALU.is_gt))
            link(V.tensor_reduce(ntile[:], more[:], X, ALU.add))
            V.tensor_scalar(skip[:], ntile[:], -1.0, float(SPAN // P), ALU.mult, ALU.add)
            link(V.tensor_tensor_scan(tile_end[:], one8[:], ntile[:], 0.0, ALU.mult, ALU.add))
            link(V.tensor_tensor(ended[:], tile_end[:, None, :].to_broadcast([1, TILES, E]),
                                 tile_no[:, :, None].to_broadcast([1, TILES, E]), ALU.is_le))
            V.tensor_reduce(expf[:], ended[:], X, ALU.add)
            link(V.tensor_tensor(skipped[:], ended[:], skip[:, None, :].to_broadcast([1, TILES, E]), ALU.mult))
            link(V.tensor_reduce(blkf[:], skipped[:], X, ALU.add))
            V.tensor_copy(pad_at[:], head[0:1, :])
            V.tensor_scalar(tile_expert[:], expf[:], float(E - 1), None, ALU.min)
            V.tensor_tensor(tile_block[:], blkf[:], tile_no[:], ALU.add).then_inc(s_tab, 1)

            def step(t, c):
                if 0 <= c <= LAST:
                    dve.wait_ge(s_silu, t + 1)
                    dve.wait_ge(s_up, t + 1)
                    at_least(dve, s_h, t - 1)
                    V.tensor_tensor(hid[:, c % 2, :], st[:, 2 + c % 2, :], sg[:, c % 2, :], ALU.mult).then_inc(s_hid, 1)
                if c + 1 <= LAST:
                    dve.wait_ge(s_ld[(c + 1) % 2], 8 * (t + 1 - (c + 1) % 2) + 16)
                    V.tensor_copy(meta[:, bass.ds(t + 1, 1), :].rearrange("p a w -> p (a w)"), xt[:, (c + 1) % 2, D:D + 2]).then_inc(s_meta, 1)
                if c >= 2:
                    dve.wait_ge(s_d, t - 1)
                    at_least(dve, s_ret[c % 2], 8 * (t - 2 - c % 2))
                    dve.wait_ge(s_meta, t - 1)
                    V.tensor_copy(ridx[:, c % 2:c % 2 + 1], meta[:, bass.ds(t - 2, 1), 1])
                    V.tensor_scalar(ysb[:, c % 2, :], work[1][:, 0:D], meta[:, bass.ds(t - 2, 1), 0], None, ALU.mult).then_inc(s_y, 1)
            pipeline(dve, step)
            for b in range(B):
                dve.wait_ge(s_yb[b], 16)
                for k in range(TOPK):
                    V.tensor_tensor(x2[:, b], x2[:, b], yb[:, LT * b:LT * b + LT, k, :], ALU.add).then_inc(s_fin, 1)
                    dve.wait_ge(s_fin, 2 * b + k + 1)


def _layout(inputs):
    import numpy as np
    f = np.float32
    x = np.ascontiguousarray(inputs["x"])
    c = np.asarray(inputs["ctx_768"])
    ctxT = np.ones((C + 1, B * M), f)
    ctxT[:C] = c.reshape(B * M, C).T
    Wq, bq = np.asarray(inputs["L0_xattn_Wq"]), np.asarray(inputs["L0_xattn_bq"])
    Wkv, bkv = np.asarray(inputs["L0_xattn_Wkv"]), np.asarray(inputs["L0_xattn_bkv"])
    wq = np.zeros((D, QD, P), f); bqs = np.zeros((P, QD), f)
    wk = np.zeros((C + 1, QD, P), f); wv = np.zeros((C + 1, D), f)
    for h in range(H):
        i, g = divmod(h, G)
        for first in (ROW_HI, ROW_LO, ROW_KLO):
            r = 32 * g + first
            wq[:, i, r:r + DH] = Wq[DH * h:DH * h + DH].T
            bqs[r:r + DH, i] = bq[DH * h:DH * h + DH]
            wk[:C, i, r:r + DH] = Wkv[2 * DH * h:2 * DH * h + DH].T
            wk[C, i, r:r + DH] = bkv[2 * DH * h:2 * DH * h + DH]
        wk[C, i, 32 * g + ROW_MAX:32 * g + ROW_MAX + 2] = 1.0
        wv[:C, DH * h:DH * h + DH] = Wkv[2 * DH * h + DH:2 * DH * h + 2 * DH].T
        wv[C, DH * h:DH * h + DH] = bkv[2 * DH * h + DH:2 * DH * h + 2 * DH]
    low = np.zeros((P, 2), f)
    for g in range(G):
        low[32 * g + ROW_LO:32 * g + ROW_LO + DH, 0] = -1.0
        low[32 * g + ROW_KLO:32 * g + ROW_KLO + DH, 1] = -1.0
    Wo = np.asarray(inputs["L0_xattn_Wo"])
    wo = np.zeros((D, D), f)
    for hf in range(2):
        for g in range(G):
            for j in range(2):
                h = G * (2 * hf + j) + g
                r = 64 * hf + (2 * g + j) * DH
                wo[r:r + DH] = Wo[:, DH * h:DH * h + DH].T
    bo = np.ascontiguousarray(np.broadcast_to(np.asarray(inputs["L0_xattn_bo"]), (P, D)))
    gateT = np.ascontiguousarray(np.asarray(inputs["L0_ffn_gate_w"]).T)
    wg, wu, wd = (np.asarray(inputs["L0_ffn_" + n]) for n in ("wg", "wu", "wd"))
    wgu = np.ascontiguousarray(np.concatenate([wg.transpose(0, 2, 1), wu.transpose(0, 2, 1)], axis=2))
    wdT = np.ascontiguousarray(wd.transpose(0, 2, 1).reshape(E, IC, P, D).transpose(0, 2, 1, 3).reshape(E, P, IC * D))
    return dict(x=x, ctxT=ctxT, wq=wq, bq=bqs, wk=wk, wv=wv, wo=wo, bo=bo, gateT=gateT, wgu=wgu, wd=wdT, low=low)


def kernel(**inputs):
    import concourse.bacc as _bacc
    from concourse.bass_utils import run_bass_kernel_spmd as _run

    nc = _bacc.Bacc("TRN2", target_bir_lowering=False, num_devices=1)
    arrays = _layout(inputs)
    args = {n: nc.dram_tensor(n + "_dram", a.shape, F32, kind="ExternalInput").ap() for n, a in arrays.items()}
    out = nc.dram_tensor("out_dram", (B, L, D), F32, kind="ExternalOutput").ap()
    xattn_moe(nc, out=out, **args)
    r = _run(nc, [{n + "_dram": a for n, a in arrays.items()}], core_ids=[0])
    return r.results[0]["out_dram"]
```

```python
from contextlib import ExitStack

import concourse.bass as bass
from concourse import mybir

ALU = mybir.AluOpType
ACT = mybir.ActivationFunctionType
F32 = mybir.dt.float32
F32R = mybir.dt.float32r
BF16 = mybir.dt.bfloat16
U32 = mybir.dt.uint32
X = mybir.AxisListType.X

P = 128
B, L, D = 4, 512, 128
LT = L // P
NT = B * LT
M, C = 77, 96
H, DH = 16, 8
G = 4
QD = H // G
E, I, TOPK = 8, 512, 2
IC = I // P
EPS = 1e-5
SCALE = float(DH) ** -0.5

ROW_HI, ROW_LO, ROW_KLO, ROW_MAX = 0, 8, 16, 24

SPAN = B * L + P
TILES = B * L * TOPK // P + E - 1
DUMMY = TILES - B * L * TOPK // P
ROWW = D + 2
RET = B * L * TOPK
LAST = TILES - 1
BEFORE = 5
STAGED = 4
WARM = 24
FILL = {"A": 8, "W": 6, "Y": 34, "G": 6, "K": 14}
FILL_TILES = 16


def xattn_moe(nc, x, ctxT, wq, bq, stack, wk, wv, wo, bo, gateT, wgu, wd, low, out):
    xg = nc.dram_tensor("xg", (E * SPAN + DUMMY * P, ROWW), F32, kind="Internal").ap()
    yr = nc.dram_tensor("yr", (RET + P, D), F32, kind="Internal").ap()

    with ExitStack() as ctx:
        def sb(name, shape, dt=F32):
            return ctx.enter_context(nc.sbuf_tensor(name, shape, dt))

        def sem(name):
            return ctx.enter_context(nc.semaphore(name))

        xb = sb("xb", [P, B, LT, D])
        ctxT_s = sb("ctxT_s", [C + 1, B * M])
        wq_s = sb("wq_s", [D, D])
        bq_s = sb("bq_s", [P, 1])
        stack_s = sb("stack_s", [P, 2, QD, P], F32R)
        wk_s = sb("wk_s", [C + 1, QD, P])
        wv_s = sb("wv_s", [C + 1, D])
        wo_s = sb("wo_s", [D, D])
        bo_s = sb("bo_s", [P, D])
        gateT_s = sb("gateT_s", [D, E])
        wgu_s = sb("wgu_s", [D, STAGED, 2 * I])
        split = sb("split", [P, E, 2, 2 * I], F32R)
        whi, wlo = split[:, :, 0], split[:, :, 1]
        split_words = split[:].rearrange("p e n w -> p (e n w)")
        KS, KS_AT = QD * B * G * M, E * 2 * 2 * I - QD * B * G * M
        wd_s = sb("wd_s", [P, E, IC * D])

        ident = sb("ident", [P, P])
        before = sb("before", [P, P], BF16)
        ones = sb("ones", [P, P], BF16)
        negpow = sb("negpow", [P, LT])
        low_rows = sb("low_rows", [P, 1])
        k_lo = low_rows[:, 0:1]
        lane = sb("lane", [P, E])
        ret_row = sb("ret_row", [P, NT, TOPK])

        stat = sb("stat", [P, LT, 6])
        mv1 = sb("mv1", [P, B, LT, 2])
        ve1 = sb("ve1", [P, B, LT])
        rstd1 = sb("rstd1", [P, B, LT])
        xnT = sb("xnT", [D, 2, L])
        qt = sb("qt", [P, 2, L])
        qhi = sb("qhi", [P, L], F32R)
        qlo = sb("qlo", [P, L], F32R)
        Q_AT = 4
        qs = [split[:, Q_AT].rearrange("p n (i l) -> p (n i) l", l=L), sb("qs_odd", [P, QD, L], F32R)]
        kr = split_words[:, 0:QD * B * M].rearrange("p (n m) -> p n m", n=QD)
        ks = split_words[:, KS_AT:KS_AT + KS].rearrange("p (i b g m) -> p i b g m", i=QD, b=B, g=G)
        vp = sb("vp", [M, B, 2, 2, G, 32])
        nmx = sb("nmx", [P, 2, LT, G, QD])
        nmp = sb("nmp", [P, 2, LT, 2, G * QD], F32R)
        nmT = sb("nmT", [2 * H, 2, L], F32R)
        ER = 4
        ex = sb("ex", [M, ER, 2, L])
        osb = sb("osb", [P, 2, L])
        stack_in = osb[:].rearrange("p a (i r) -> p a i r", r=P)
        rd = sb("rd", [P, 2, LT, 2 * G])
        an = sb("an", [P, LT, 2, 2 * G, DH])
        anT = sb("anT", [D, L])
        x2 = sb("x2", [P, B, LT, D])
        stat2 = sb("stat2", [P, LT, 6])
        mv2 = sb("mv2", [P, LT, 2])
        ve2 = sb("ve2", [P, LT])
        rstd2 = sb("rstd2", [P, LT])
        xs = sb("xs", [P, NT, TOPK, ROWW])
        xn = xs[:, :, 0, 0:D].rearrange("p (b t) d -> p b t d", b=B)
        yb = xs[:].rearrange("p t k w -> p (t k w)")[:, 0:NT * TOPK * D].rearrange("p (t k d) -> p t k d", k=TOPK, d=D)
        x2T = sb("x2T", [D, L])
        lg = sb("lg", [P, LT, E])
        top = sb("top", [P, LT, 8])
        topi = sb("topi", [P, LT, 8], U32)
        topf = sb("topf", [P, LT, TOPK])
        pick = sb("pick", [P, TOPK, LT, E])
        chosen = sb("chosen", [P, LT, E], BF16)
        gap = sb("gap", [P, LT])
        gexp = sb("gexp", [P, LT])
        gden = sb("gden", [P, LT])
        head = sb("head", [P, E])
        pos = sb("pos", [P, LT, E])
        posk = sb("posk", [P, TOPK, LT, E])
        rowf = sb("rowf", [P, TOPK, LT])
        row = sb("row", [P, NT, TOPK], U32)

        base = sb("base", [P, E])
        steps128 = sb("steps128", [1, NT])
        tile_no = sb("tile_no", [1, TILES])
        count = sb("count", [1, E])
        more = sb("more", [1, E, NT])
        ntile = sb("ntile", [1, E])
        one8 = sb("one8", [1, E])
        tile_end = sb("tile_end", [1, E])
        ended = sb("ended", [1, TILES, E])
        skip = sb("skip", [1, E])
        skipped = sb("skipped", [1, TILES, E])
        expf = sb("expf", [1, TILES])
        blkf = sb("blkf", [1, TILES])
        tile_expert = sb("tile_expert", [1, TILES], U32)
        tile_block = sb("tile_block", [1, TILES], U32)
        pad_at = sb("pad_at", [1, E], U32)
        padrow = sb("padrow", [P, ROWW])
        warm = sb("warm", [P, 1])
        xt = xb[:, 0].rearrange("p t d -> p (t d)")[:, 0:2 * ROWW].rearrange("p (n w) -> p n w", n=2)
        ysb = xb[:, 2, 0:2]
        ehi, elo = qs[1][:, 0, 0:2 * P].rearrange("p (n m) -> p n m", n=2), qs[1][:, 1, 0:2 * P].rearrange("p (n m) -> p n m", n=2)
        meta = sb("meta", [P, TILES, 2])
        sg, hid, hT = qt, osb, xnT
        ridx = sb("ridx", [P, 2], U32)

        work = [ctx.enter_context(nc.psum_tensor(f"work{n}", [P, 512], F32)) for n in range(3)]
        opv = ctx.enter_context(nc.psum_tensor("opv", [P, 512], F32))
        st = ctx.enter_context(nc.psum_tensor("st", [P, G, 512], F32))
        hT_bank = [opv, work[2]]

        s_x = [sem(f"s_xin{b}") for b in range(B)]
        s_wk = sem("s_wk"); s_wq = sem("s_wq"); s_wvo = sem("s_wvo"); s_wgu = [sem(f"s_wgu{e}") for e in range(E)]; s_wd = sem("s_wd")
        s_id = sem("s_id"); s_cst = sem("s_cst"); s_pool = sem("s_pool")
        s_dve = sem("s_dve")
        s_stat1 = sem("s_stat1"); s_rstd1 = sem("s_rstd1"); s_xn = sem("s_xn"); s_xb = sem("s_xb")
        s_kps = sem("s_kps"); s_kr = sem("s_kr"); s_ksr = sem("s_ksr"); s_kz = sem("s_kz")
        s_ks = sem("s_ks"); s_ks2 = sem("s_ks2")
        s_vps = sem("s_vps"); s_vp = sem("s_vp")
        s_xT = sem("s_xT"); s_xnT = sem("s_xnT")
        s_stack = sem("s_stack"); s_pq = sem("s_pq"); s_qlo = sem("s_qlo"); s_q = sem("s_q"); s_qt = sem("s_qt"); s_qs = sem("s_qs")
        s_l = sem("s_l"); s_mx = sem("s_mx"); s_nt = sem("s_nt"); s_nmp = sem("s_nmp"); s_nm = sem("s_nm")
        s_nmd = [sem(f"s_nmd{n}") for n in range(2)]
        s_s = sem("s_s"); s_e = sem("s_e"); s_pv = sem("s_pv"); s_osb = sem("s_osb")
        s_ot = sem("s_ot"); s_an = sem("s_an"); s_at = sem("s_at"); s_anT = sem("s_anT")
        s_wo = sem("s_wo"); s_x2 = sem("s_x2"); s_stat2 = sem("s_stat2"); s_rstd2 = sem("s_rstd2")
        s_xs = sem("s_xs"); s_x2t = sem("s_x2t"); s_x2T = sem("s_x2T")
        s_g = sem("s_g"); s_lg = sem("s_lg"); s_gap = sem("s_gap"); s_gexp = sem("s_gexp"); s_prob = sem("s_prob")
        s_chosen = sem("s_chosen"); s_rk = sem("s_rk"); s_pos = sem("s_pos"); s_row = sem("s_row")
        s_disp = sem("s_disp"); s_out = sem("s_out")
        s_warm = sem("s_warm"); s_pad = sem("s_pad"); s_padw = sem("s_padw"); s_tab = sem("s_tab")
        s_ld = [sem(f"s_ld{n}") for n in range(2)]
        s_meta = sem("s_meta")
        s_t = sem("s_t"); s_eT = sem("s_eT"); s_elo = sem("s_elo"); s_whi = sem("s_whi"); s_wlo = sem("s_wlo"); s_wlo2 = sem("s_wlo2"); s_gate = sem("s_gate"); s_up = sem("s_up")
        s_silu = sem("s_silu"); s_hid = sem("s_hid"); s_h = sem("s_h"); s_hT = sem("s_hT")
        s_d = sem("s_d"); s_y = sem("s_y")
        s_ret = [sem(f"s_ret{n}") for n in range(2)]
        s_yb = [sem(f"s_yb{n}") for n in range(B)]
        s_fin = sem("s_fin")

        PAIRS, EARLY = H // 2, 3
        split_at = dict(zip((3, 6, 7, 9, B * PAIRS - 6), range(Q_AT + 1)))
        ON_POOL = Q_AT

        def to_scores(b):
            rest = ([("Q", b, i) for i in range(QD)] +
                    [("R", b, lt, i) for lt in range(LT) for i in range(QD)] + [("T", b)])
            at = 12 if b else 21
            return rest[:at] + [("X", b + 1), ("P", b + 1)] * (b + 1 < B) + rest[at:]

        def from_values(b):
            return [[("O", b, 0)], [("O", b, 1)], [("A", b)], [("W", b)], [], [("Y", b)], [("G", b)], [("K", b)]]

        steps = [("M", 0), ("KP", 0), ("N", 0), ("KP", 1), ("KP", 2), ("KP", 3), ("X", 0), ("KB", 0), ("P", 0), ("KB", 1), ("KB", 2), ("KB", 3)]
        first = to_scores(0)
        steps += first[:1] + [("M", 1)] + first[1:4] + [("N", 1)] + first[4:] + [("VP", 0)]
        queue = []
        for n in range(B * PAIRS + 1):
            b, j = divmod(n, PAIRS)
            if n < B * PAIRS:
                steps.append(("S", b, j))
            if n == 0 or (n + EARLY) % PAIRS == 0:
                nxt = (n + EARLY) // PAIRS + 1
                if nxt < B:
                    queue += to_scores(nxt)
            ahead = 4 if j in (2, 4, 6) else 3
            steps += queue[:ahead]
            queue = queue[ahead:]
            if n:
                steps.append(("V", (n - 1) // PAIRS, (n - 1) % PAIRS))
            if n in (1, 4):
                steps.append(("M", 2 + n // 4))
            if n in (2, 5):
                steps.append(("N", 2 + n // 4))
            if n in split_at:
                steps.append(("E", split_at[n]))
            if b and n < B * PAIRS:
                steps += from_values(b - 1)[j]
        for s in sum(from_values(B - 1), []):
            steps += [("F", FILL.get(s[0], 0)), s]
        late = [("E", e) for e in range(Q_AT + 1, E)]

        reader = {"X": (s_xnT, lambda b: b + 1), "P": (s_qt, lambda b: b + 1), "Q": (s_qs, lambda b, i: QD * b + i + 1),
                  "R": (s_mx, lambda b, lt, i: NT * b + QD * lt + i + 1), "T": (s_nm, lambda b: b + 1),
                  "O": (s_an, lambda b, h: 2 * b + h + 1), "A": (s_anT, lambda b: b + 1),
                  "W": (s_x2, lambda b: b + 1), "Y": (s_x2T, lambda b: b + 1),
                  "G": (s_lg, lambda b: b + 1), "K": (s_pos, lambda b: b + 1)}
        uses = [s for s in steps if s[0] in reader]
        turn = {s: n for n, s in enumerate(uses)}

        def claim(eng, s):
            n = turn[s]
            if n >= 3:
                who, value = reader[uses[n - 3][0]]
                eng.wait_ge(who, value(*uses[n - 3][1:]))
            return work[n % 3]

        FIRST, STOP, UNROLL = 6, LAST, 4
        assert (STOP - FIRST) % UNROLL == 0 and UNROLL % 2 == 0

        def pipeline(eng, step):
            for t in range(-1, FIRST):
                step(t, t)
            with eng.Fori(0, (STOP - FIRST) // UNROLL) as i:
                for c in range(UNROLL):
                    step(UNROLL * i + FIRST + c, FIRST + c)
            for t in range(STOP, LAST + 3):
                step(t, t)

        def at_least(eng, s, value):
            if not isinstance(value, int) or value > 0:
                eng.wait_ge(s, value)

        block = ctx.enter_context(nc.Block())

        @block.sync
        def _(sp):
            def load_x(b):
                sp.dma_start(xb[:, b], x[b].rearrange("(t p) d -> p t d", p=P)).then_inc(s_x[b], 16)

            load_x(0)
            for dst, src in ((ctxT_s, ctxT), (wk_s, wk), (low_rows, low)):
                sp.dma_start(dst[:], src).then_inc(s_wk, 16)
            for dst, src in ((wq_s, wq), (bq_s, bq), (stack_in, stack)):
                sp.dma_start(dst if dst is stack_in else dst[:], src).then_inc(s_wq, 16)
            for b in range(1, B):
                load_x(b)
            for dst, src in ((wv_s, wv), (wo_s, wo), (bo_s, bo), (gateT_s, gateT)):
                sp.dma_start(dst[:], src).then_inc(s_wvo, 16)
            def load_wgu(e):
                sp.dma_start(wgu_s[:, e % STAGED, :], wgu[e]).then_inc(s_wgu[e], 16)

            for e in range(STAGED):
                load_wgu(e)
            for e in range(E):
                sp.dma_start(wd_s[:, e, :], wd[e]).then_inc(s_wd, 16)
            sp.wait_ge(s_pad, 1)
            sp.dma_start(xg[E * SPAN:E * SPAN + P * DUMMY, :].rearrange("(n p) w -> p n w", p=P),
                         padrow[:, None, :].to_broadcast([P, DUMMY, ROWW])).then_inc(s_padw, 16)
            for b in range(B):
                sp.wait_ge(s_nm, b + 1)
                for n in range(2):
                    sp.dma_start(qs[b % 2][ROW_MAX + n:P:32, :, :].bitcast(F32),
                                 nmT[H * n:H * n + H, b % 2, :].bitcast(F32)).then_inc(s_nmd[b % 2], 16)
                if b == 1:
                    for e in range(STAGED, E):
                        sp.wait_ge(s_wlo, e - STAGED + 1)
                        load_wgu(e)
            sp.wait_ge(s_tab, 1)
            for e in range(0, E, 2):
                at = sp.value_load(pad_at[0:1, e:e + 1], min_val=e * SPAN, max_val=e * SPAN + B * L)
                sp.dma_start(xg[bass.ds(at, P), :], padrow[:]).then_inc(s_padw, 16)
            sp.wait_ge(s_padw, 16 * (E + 1))
            sp.wait_ge(s_disp, 16 * NT * TOPK)
            blocks = xg.rearrange("(n p) w -> n p w", p=P)

            def load(t, c):
                blk = sp.value_load(tile_block[0:1, bass.ds(t, 1)], min_val=0, max_val=E * SPAN // P + DUMMY - 1)
                at_least(sp, s_t, t - 1)
                at_least(sp, s_meta, t - 1)
                sp.dma_start(xt[:, c % 2, :],
                             blocks[bass.ds(blk, 1)].rearrange("a p w -> (a p) w")).then_inc(s_ld[c % 2], 16)

            load(0, 0)
            load(1, 1)
            with sp.Fori(1, (TILES - 1) // 2) as i:
                for c in range(2):
                    load(2 * i + c, 2 + c)
            load(LAST, LAST)
            for n in range(2):
                sp.wait_ge(s_ret[n], 16 * ((TILES + 1 - n) // 2))
            for b in range(B):
                sp.dma_start(yb[:, LT * b:LT * b + LT].rearrange("p t k d -> p t (k d)"),
                             yr[TOPK * L * b:TOPK * L * (b + 1), :].rearrange("(t p k) d -> p t (k d)", p=P, k=TOPK)).then_inc(s_yb[b], 16)
            for b in range(B):
                sp.wait_ge(s_fin, 2 * b + 2)
                sp.dma_start(out[b].rearrange("(t p) d -> p t d", p=P), x2[:, b]).then_inc(s_out, 16)
            sp.wait_ge(s_out, 16 * B)

        @block.gpsimd
        def _(pool):
            pool.memset(ident[:], 0.0).then_inc(s_pool, 1)
            pool.memset(before[:], 1.0).then_inc(s_pool, 1)
            pool.wait_ge(s_pool, 1)
            pool.affine_select(out=ident[:], in_=ident[:], compare_op=ALU.not_equal, fill=1.0, base=0,
                               pattern=[[-1, P]], channel_multiplier=1).then_inc(s_id, 1)
            pool.memset(negpow[:], -0.5).then_inc(s_pool, 1)
            pool.memset(vp[:], 0.0).then_inc(s_pool, 1)
            done = 4

            def rstd_1(b):
                pool.wait_ge(s_stat1, b + 1)
                pool.tensor_tensor(rstd1[:, b], ve1[:, b], negpow[:], ALU.pow).then_inc(s_rstd1, 1)

            pool.wait_ge(s_pool, 3)
            rstd_1(0)
            pool.wait_ge(s_pool, done)
            for j in range(2):
                pool.memset(vp[:, :, :, j, :, 16 * j + DH:16 * j + DH + 1], 1.0).then_inc(s_cst, 1)
            pool.affine_select(out=before[:], in_=before[:], compare_op=ALU.is_gt, fill=0.0, base=0,
                               pattern=[[1, P]], channel_multiplier=-1).then_inc(s_cst, 1)
            pool.memset(ones[:], 1.0).then_inc(s_cst, 1)
            pool.iota(lane[:], [[1, E]], base=0, channel_multiplier=0,
                      allow_small_or_imprecise_dtypes=True).then_inc(s_cst, 1)
            pool.iota(head[:], [[SPAN, E]], base=0, channel_multiplier=0,
                      allow_small_or_imprecise_dtypes=True).then_inc(s_cst, 1)
            pool.iota(ret_row[:], [[TOPK * P, NT], [1, TOPK]], base=0, channel_multiplier=TOPK,
                      allow_small_or_imprecise_dtypes=True).then_inc(s_cst, 1)
            rstd_1(1)
            pool.memset(padrow[:], 0.0).then_inc(s_pool, 1)
            done += 1
            pool.wait_ge(s_pool, done)
            pool.iota(padrow[:, D + 1:D + 2], [[0, 1]], base=RET, channel_multiplier=1,
                      allow_small_or_imprecise_dtypes=True).then_inc(s_pad, 1)
            pool.iota(base[:], [[SPAN, E]], base=0, channel_multiplier=0,
                      allow_small_or_imprecise_dtypes=True).then_inc(s_cst, 1)
            pool.iota(steps128[:], [[P, NT]], base=0, channel_multiplier=0,
                      allow_small_or_imprecise_dtypes=True).then_inc(s_cst, 1)
            pool.iota(tile_no[:], [[1, TILES]], base=0, channel_multiplier=0,
                      allow_small_or_imprecise_dtypes=True).then_inc(s_cst, 1)
            pool.memset(one8[:], 1.0).then_inc(s_cst, 1)
            pool.wait_ge(s_wvo, 16 * 4)
            for b in range(B):
                if b >= 2:
                    rstd_1(b)
                pool.wait_ge(s_xn, b + 1)
                pool.tensor_tensor(xb[:, b], xb[:, b], bo_s[:, None, :].to_broadcast([P, LT, D]), ALU.add).then_inc(s_xb, 1)
                for e in ((), (), (0,), range(1, ON_POOL))[b]:
                    pool.wait_ge(s_whi, e + 1)
                    pool.tensor_tensor(wlo[:, e], wgu_s[:, e], whi[:, e].bitcast(F32), ALU.subtract).then_inc(s_wlo, 1)

            def rstd_2(b):
                pool.wait_ge(s_stat2, b + 1)
                if b:
                    pool.wait_ge(s_xs, b)
                pool.tensor_tensor(rstd2[:], ve2[:], negpow[:], ALU.pow).then_inc(s_rstd2, 1)

            def dispatch(b, n):
                t, k = LT * b + n // TOPK, n % TOPK
                pool.indirect_dma_start(out=xg, out_offset=bass.IndirectOffsetOnAxis(ap=row[:, t, k:k + 1], axis=0),
                                        in_=xs[:, t, k, :], in_offset=None).then_inc(s_disp, 16)

            for b in range(B):
                if b < B - 1:
                    rstd_2(b)
                pool.wait_ge(s_xs, b + 1)
                pool.tensor_copy(xs[:, LT * b:LT * b + LT, 1, 0:D], xs[:, LT * b:LT * b + LT, 0, 0:D]).then_inc(s_pool, 1)
                done += 1
                pool.wait_ge(s_pool, done)
                pool.wait_ge(s_prob, b + 1)
                pool.wait_ge(s_row, b + 1)
                for n in range(LT * TOPK):
                    if b == B - 2 and n == BEFORE:
                        rstd_2(b + 1)
                    dispatch(b, n)

            last_row = pool.to_reg(RET - 1)
            def step(t, c):
                if c >= 2:
                    pool.wait_ge(s_y, t - 1)
                    pool.nop(nofuse=True)
                    pool.indirect_dma_start(out=yr, out_offset=bass.IndirectOffsetOnAxis(ap=ridx[:, c % 2:c % 2 + 1], axis=0),
                                            in_=ysb[:, c % 2, :], in_offset=None,
                                            bounds_check=last_row, oob_is_err=False).then_inc(s_ret[c % 2], 16)
            pipeline(pool, step)

        @block.tensor
        def _(pe):
            pe.wait_ge(s_id, 1)
            def fill(count):
                for n in range(count):
                    nc.tensor.transpose(st[:, 3, 0:P], ident[:], ident[:])

            fill(WARM)
            for s in steps:
                kind = s[0]
                b = s[1]
                if kind in reader:
                    w = claim(pe, s)
                if kind == "F":
                    fill(s[1])
                elif kind == "KP":
                    i = s[1]
                    pe.wait_ge(s_wk, 16 * 3)
                    nc.tensor.matmul(st[:, i, 0:B * M], wk_s[:, i, :], ctxT_s[:], start=True, stop=True).then_inc(s_kps, 1)
                elif kind == "VP":
                    pe.wait_ge(s_wvo, 16 * 4)
                    for n in range(B):
                        last = nc.tensor.matmul(opv[0:M, D * n:D * n + D], ctxT_s[:, M * n:M * n + M], wv_s[:], start=True, stop=True)
                    last.then_inc(s_vps, 1)
                elif kind == "X":
                    pe.wait_ge(s_xn, b + 1)
                    for t in range(LT):
                        last = nc.tensor.transpose(w[:, P * t:P * t + P], xn[:, b, t, :], ident[:])
                    last.then_inc(s_xT, 1)
                elif kind == "P":
                    pe.wait_ge(s_xnT, b + 1)
                    pe.wait_ge(s_wq, 16 * 3)
                    nc.tensor.matmul(w[:], wq_s[:], xnT[:, b % 2, :], start=True, stop=True).then_inc(s_pq, 1)
                elif kind == "Q":
                    i = s[2]
                    pe.wait_ge(s_stack, 1)
                    pe.wait_ge(s_qlo, b + 1)
                    nc.tensor.matmul(w[:], stack_s[:, 0, i, :], qhi[:], start=True, stop=False)
                    nc.tensor.matmul(w[:], stack_s[:, 1, i, :], qlo[:], start=False, stop=True).then_inc(s_q, 1)
                elif kind == "R":
                    lt, i = s[2], s[3]
                    pe.wait_ge(s_qs, QD * b + i + 1)
                    if b == 0:
                        pe.wait_ge(s_ks, 2 * (i + 1))
                        pe.wait_ge(s_ks2, 2 * (i + 1))
                    nc.tensor.matmul(w[:, 0:G * M], qs[b % 2][:, i, P * lt:P * lt + P],
                                     ks[:, i, b].rearrange("p g m -> p (g m)"), start=True, stop=True).then_inc(s_l, 1)
                elif kind == "T":
                    pe.wait_ge(s_nmp, b + 1)
                    for t in range(LT):
                        last = nc.tensor.transpose(w[0:2 * H, P * t:P * t + P],
                                                   nmp[:, b % 2, t].bitcast(F32).rearrange("p a h -> p (a h)"), ident[:])
                    last.then_inc(s_nt, 1)
                elif kind == "S":
                    n = PAIRS * b + s[2]
                    i = s[2] // 2
                    pe.wait_ge(s_nmd[b % 2], 32 * (b // 2 + 1))
                    if n >= 2:
                        pe.wait_ge(s_e, n - 1)
                    for g in range(2 * (n % 2), 2 * (n % 2) + 2):
                        last = nc.tensor.matmul(st[0:M, g, :], ks[:, i, b, g, :], qs[b % 2][:, i, :], start=True, stop=True)
                    last.then_inc(s_s, 1)
                elif kind == "V":
                    n = PAIRS * b + s[2]
                    i = s[2] // 2
                    pe.wait_ge(s_vp, 1)
                    if s[2] % (PAIRS // 2) == 0 and n:
                        pe.wait_ge(s_osb, n // (PAIRS // 2))
                    pe.wait_ge(s_e, n + 1)
                    for g in range(2 * (n % 2), 2 * (n % 2) + 2):
                        last = nc.tensor.matmul(opv[32 * g:32 * g + 32, :], vp[:, b, i // 2, i % 2, g, :],
                                                ex[:, n % ER, g % 2, :], start=(i % 2 == 0), stop=(i % 2 == 1),
                                                tile_position=(0, 32 * g))
                    last.then_inc(s_pv, 1)
                elif kind == "O":
                    hf = s[2]
                    pe.wait_ge(s_osb, 2 * b + hf + 1)
                    for t in range(LT):
                        last = nc.tensor.transpose(w[:, P * t:P * t + P], osb[:, hf, P * t:P * t + P], ident[:])
                    last.then_inc(s_ot, 1)
                elif kind == "A":
                    pe.wait_ge(s_an, 2 * (b + 1))
                    for t in range(LT):
                        last = nc.tensor.transpose(w[:, P * t:P * t + P],
                                                   an[:, t].rearrange("p a b d -> p (a b d)"), ident[:])
                    last.then_inc(s_at, 1)
                elif kind == "W":
                    pe.wait_ge(s_anT, b + 1)
                    for t in range(LT):
                        last = nc.tensor.matmul(w[:, P * t:P * t + P], anT[:, P * t:P * t + P], wo_s[:], start=True, stop=True)
                    last.then_inc(s_wo, 1)
                elif kind == "Y":
                    pe.wait_ge(s_xs, b + 1)
                    for t in range(LT):
                        last = nc.tensor.transpose(w[:, P * t:P * t + P], xs[:, LT * b + t, 0, 0:D], ident[:])
                    last.then_inc(s_x2t, 1)
                elif kind == "G":
                    pe.wait_ge(s_x2T, b + 1)
                    for t in range(LT):
                        last = nc.tensor.matmul(w[:, E * t:E * t + E], x2T[:, P * t:P * t + P], gateT_s[:], start=True, stop=True)
                    last.then_inc(s_g, 1)
                elif kind == "K":
                    pe.wait_ge(s_chosen, b + 1)
                    pe.wait_ge(s_cst, 11)
                    nc.tensor.matmul(w[:, 0:LT * E], before[:], chosen[:].rearrange("p t e -> p (t e)"), start=True, stop=False)
                    for t in range(LT - 1):
                        nc.tensor.matmul(w[:, E * (t + 1):LT * E], ones[:],
                                         chosen[:, t:t + 1, :].to_broadcast([P, LT - 1 - t, E]),
                                         start=False, stop=(t == LT - 2))
                    for t in range(LT):
                        last = nc.tensor.matmul(w[:, LT * E:LT * E + E], ones[:], chosen[:, t, :],
                                                start=(t == 0), stop=(t == LT - 1))
                    last.then_inc(s_rk, 1)

            pe.wait_ge(s_e, PAIRS * B)
            pe.wait_ge(s_osb, 2 * B)
            pe.wait_ge(s_pos, B)
            pe.wait_ge(s_wd, 16 * E)
            pe.wait_ge(s_wlo, ON_POOL)
            pe.wait_ge(s_wlo2, E - ON_POOL)
            pe.wait_ge(s_tab, 1)
            pe.wait_ge(s_padw, 16 * (E + 1))
            fill(FILL_TILES)

            down_expert = [pe.alloc_register(f"down_expert{n}") for n in range(2)]
            expert = {}

            def step(t, c):
                if 0 <= c <= LAST:
                    e = pe.value_load(tile_expert[0:1, bass.ds(t, 1)], min_val=0, max_val=E - 1)
                    expert[c] = e
                    pe.wait_ge(s_elo, t + 1)
                    for n, done in ((0, s_gate), (1, s_up)):
                        whi_e, wlo_e = (w[:, bass.ds(e, 1), I * n:I * n + I].rearrange("p a n -> p (a n)") for w in (whi, wlo))
                        nc.tensor.matmul(st[:, 2 * n + c % 2, :], ehi[:, c % 2, :], whi_e, start=True, stop=False)
                        nc.tensor.matmul(st[:, 2 * n + c % 2, :], ehi[:, c % 2, :], wlo_e, start=False, stop=False)
                        nc.tensor.matmul(st[:, 2 * n + c % 2, :], elo[:, c % 2, :], whi_e, start=False, stop=True).then_inc(done, 1)
                if c + 1 <= LAST:
                    pe.wait_ge(s_ld[(c + 1) % 2], 8 * (t + 1 - (c + 1) % 2) + 16)
                    nc.tensor.transpose(work[0][:, 0:P], xt[:, (c + 1) % 2, 0:D], ident[:]).then_inc(s_t, 1)
                if 1 <= c <= LAST + 1:
                    pe.wait_ge(s_hid, t)
                    for n in range(IC):
                        last = nc.tensor.transpose(hT_bank[(c + 1) % 2][:, P * n:P * n + P], hid[:, (c + 1) % 2, P * n:P * n + P], ident[:])
                    last.then_inc(s_h, 1)
                if c >= 2:
                    if isinstance(t, int) and STOP <= c < STOP + 2:
                        down_e = pe.value_load(tile_expert[0:1, t - 2:t - 1], min_val=0, max_val=E - 1)
                    elif not isinstance(t, int) and c < FIRST + 2:
                        down_e = bass.RuntimeValue.of_register_unchecked(down_expert[c % 2], min_val=0, max_val=E - 1)
                    else:
                        down_e = expert[c - 2]
                    pe.wait_ge(s_hT, t - 1)
                    at_least(pe, s_y, t - 2)
                    for n in range(IC):
                        last = nc.tensor.matmul(work[1][:, 0:D], hT[:, c % 2, P * n:P * n + P],
                                                wd_s[:, bass.ds(down_e, 1), D * n:D * n + D].rearrange("p a n -> p (a n)"),
                                                start=(n == 0), stop=(n == IC - 1))
                    last.then_inc(s_d, 1)
                if c in (FIRST - 2, FIRST - 1, FIRST + UNROLL - 2, FIRST + UNROLL - 1):
                    pe.reg_mov(down_expert[c % 2], e)
            pipeline(pe, step)

        @block.scalar
        def _(act):
            def high_part(e):
                act.wait_ge(s_wgu[e], 16)
                if e == 0:
                    act.wait_ge(s_ks, 2 * QD)
                    act.wait_ge(s_ks2, 2 * QD)
                elif e == Q_AT:
                    act.wait_ge(s_s, PAIRS * (B - 1))
                elif e > Q_AT:
                    act.wait_ge(s_s, PAIRS * B)
                nc.scalar.copy(whi[:, e], wgu_s[:, e % STAGED]).then_inc(s_whi, 1)

            act.wait_ge(s_wq, 16 * 3)
            nc.scalar.copy(stack_s[:], stack_in).then_inc(s_stack, 1)
            for s in steps:
                kind = s[0]
                b = s[1]
                w = work[turn[s] % 3] if s in turn else None
                if kind == "KP":
                    i = s[1]
                    act.wait_ge(s_kps, i + 1)
                    nc.scalar.copy(kr[:, i, :], st[:, i, 0:B * M]).then_inc(s_kr, 1)
                elif kind == "KB":
                    i = s[1]
                    act.wait_ge(s_kz, i + 1)
                    act.wait_ge(s_ksr, i + 1)
                    for g in range(2, G):
                        r = slice(32 * g, 32 * g + 32)
                        nc.scalar.copy(ks[r, i, :, g, :], kr[r, i, :].bitcast(F32).rearrange("p (b m) -> p b m", b=B)).then_inc(s_ks2, 1)
                elif kind == "VP":
                    act.wait_ge(s_vps, 1)
                    act.wait_ge(s_cst, 2)
                    for hf in range(2):
                        for j in range(2):
                            last = nc.scalar.copy(vp[:, :, hf, j, :, 16 * j:16 * j + DH],
                                                  opv[0:M, :].rearrange("m (b q g d) -> m b q g d", b=B, q=QD, g=G)[:, :, 2 * hf + j])
                    last.then_inc(s_vp, 1)
                elif kind == "E":
                    high_part(b)
                elif kind == "X":
                    act.wait_ge(s_xT, b + 1)
                    if b >= 2:
                        act.wait_ge(s_pq, b - 1)
                    nc.scalar.copy(xnT[:, b % 2, :], w[:]).then_inc(s_xnT, 1)
                elif kind == "T":
                    act.wait_ge(s_nt, b + 1)
                    if b >= 2:
                        act.wait_ge(s_nmd[b % 2], 32 * (b // 2))
                    nc.scalar.copy(nmT[:, b % 2, :], w[0:2 * H, :]).then_inc(s_nm, 1)
                elif kind == "P":
                    act.wait_ge(s_pq, b + 1)
                    if b:
                        act.wait_ge(s_q, QD * b)
                        act.wait_ge(s_qlo, b)
                    nc.scalar.activation(qhi[:], w[:], ACT.Identity, bias=bq_s[:])
                    nc.scalar.activation(qt[:, 0, :], w[:], ACT.Identity, bias=bq_s[:]).then_inc(s_qt, 1)
                elif kind == "Q":
                    i = s[2]
                    act.wait_ge(s_q, QD * b + i + 1)
                    if b >= 2:
                        act.wait_ge(s_s, PAIRS * (b - 2) + 2 * i + 2)
                    nc.scalar.copy(qs[b % 2][:, i, :], w[:]).then_inc(s_qs, 1)
                elif kind == "S":
                    n = PAIRS * b + s[2]
                    act.wait_ge(s_s, n + 1)
                    if n >= ER:
                        act.wait_ge(s_pv, n - ER + 1)
                    nc.scalar.activation(ex[:, n % ER], st[0:M, 2 * (n % 2):2 * (n % 2) + 2, :], ACT.Exp, scale=SCALE).then_inc(s_e, 1)
                elif kind == "V" and s[2] % (PAIRS // 2) == PAIRS // 2 - 1:
                    hf = s[2] // (PAIRS // 2)
                    act.wait_ge(s_pv, PAIRS * b + s[2] + 1)
                    if b:
                        act.wait_ge(s_ot, 2 * (b - 1) + hf + 1)
                    nc.scalar.copy(osb[:, hf, :], opv[:]).then_inc(s_osb, 1)
                elif kind == "A":
                    act.wait_ge(s_at, b + 1)
                    if b:
                        act.wait_ge(s_wo, b)
                    nc.scalar.copy(anT[:], w[:]).then_inc(s_anT, 1)
                elif kind == "Y":
                    act.wait_ge(s_x2t, b + 1)
                    if b:
                        act.wait_ge(s_g, b)
                    nc.scalar.copy(x2T[:], w[:]).then_inc(s_x2T, 1)
                elif kind == "G":
                    act.wait_ge(s_gap, b + 1)
                    nc.scalar.activation(gexp[:], gap[:], ACT.Exp).then_inc(s_gexp, 1)

            for s in late:
                high_part(s[1])
            act.wait_ge(s_pad, 1)
            nc.scalar.activation(warm[:], padrow[:, 0:1], ACT.Silu).then_inc(s_warm, 1)
            act.wait_ge(s_tab, 1)
            for e in range(1, E, 2):
                at = act.value_load(pad_at[0:1, e:e + 1], min_val=e * SPAN, max_val=e * SPAN + B * L)
                act.dma_start(xg[bass.ds(at, P), :], padrow[:]).then_inc(s_padw, 16)

            def step(t, c):
                if 0 <= c <= LAST:
                    act.wait_ge(s_gate, t + 1)
                    at_least(act, s_hid, t - 1)
                    nc.scalar.activation(sg[:, c % 2, :], st[:, c % 2, :], ACT.Silu).then_inc(s_silu, 1)
                if c + 1 <= LAST:
                    act.wait_ge(s_t, t + 2)
                    at_least(act, s_up, t)
                    nc.scalar.copy(ehi[:, (c + 1) % 2, :], work[0][:, 0:P]).then_inc(s_eT, 1)
                if 1 <= c <= LAST + 1:
                    act.wait_ge(s_h, t)
                    at_least(act, s_d, t - 2)
                    nc.scalar.copy(hT[:, (c + 1) % 2, :], hT_bank[(c + 1) % 2][:]).then_inc(s_hT, 1)
            pipeline(act, step)

        @block.vector
        def _(dve):
            chain = [0]

            def link(ins):
                chain[0] += 1
                ins.then_inc(s_dve, 1)
                dve.wait_ge(s_dve, chain[0])

            V = nc.vector

            def stats1(b):
                dve.wait_ge(s_x[b], 16)
                for t in range(LT):
                    ins = V.bn_stats(stat[:, t, :], xb[:, b, t, :])
                link(ins)
                for t in range(LT):
                    ins = V.bn_aggr(mv1[:, b, t, :], stat[:, t, :])
                link(ins)
                V.tensor_scalar(ve1[:, b], mv1[:, b, :, 1], EPS, None, ALU.add).then_inc(s_stat1, 1)

            def norm1(b):
                dve.wait_ge(s_stat1, b + 1)
                dve.wait_ge(s_rstd1, b + 1)
                for t in range(LT):
                    ins = V.tensor_scalar(xn[:, b, t, :], xb[:, b, t, :], mv1[:, b, t, 0:1], rstd1[:, b, t:t + 1],
                                          ALU.subtract, ALU.mult)
                ins.then_inc(s_xn, 1)

            def low_part(e):
                dve.wait_ge(s_whi, e + 1)
                V.tensor_tensor(wlo[:, e], wgu_s[:, e % STAGED], whi[:, e].bitcast(F32), ALU.subtract).then_inc(s_wlo2, 1)

            for i in range(QD):
                V.memset(ks[:, i].rearrange("p b g m -> p (b g m)").bitcast(F32), 0.0).then_inc(s_kz, 1)
            for s in steps:
                kind = s[0]
                b = s[1]
                w = work[turn[s] % 3] if s in turn else None
                if kind == "M":
                    stats1(b)
                elif kind == "N":
                    norm1(b)
                elif kind == "E" and b >= ON_POOL:
                    low_part(b)
                elif kind == "KP":
                    i = s[1]
                    dve.wait_ge(s_kr, i + 1)
                    dve.wait_ge(s_wk, 16 * 3)
                    V.scalar_tensor_tensor(kr[:, i, :], kr[:, i, :].bitcast(F32), k_lo, st[:, i, 0:B * M],
                                           ALU.mult, ALU.add).then_inc(s_ksr, 1)
                elif kind == "KB":
                    i = s[1]
                    dve.wait_ge(s_kz, i + 1)
                    dve.wait_ge(s_ksr, i + 1)
                    for g in range(2):
                        r = slice(32 * g, 32 * g + 32)
                        V.tensor_copy(ks[r, i, :, g, :], kr[r, i, :].bitcast(F32).rearrange("p (b m) -> p b m", b=B)).then_inc(s_ks, 1)
                elif kind == "P":
                    dve.wait_ge(s_qt, b + 1)
                    V.tensor_tensor(qlo[:], qt[:, 0, :], qhi[:].bitcast(F32), ALU.subtract).then_inc(s_qlo, 1)
                elif kind == "R":
                    lt, i = s[2], s[3]
                    n = NT * b + QD * lt + i
                    dve.wait_ge(s_l, n + 1)
                    V.tensor_reduce(nmx[:, b % 2, lt, :, i], w[:, 0:G * M].rearrange("p (g m) -> p g m", g=G),
                                    X, ALU.max, negate=True).then_inc(s_mx, 1)
                elif kind == "T":
                    m = nmx[:, b % 2].rearrange("p t g i -> p t (g i)")
                    dve.wait_ge(s_mx, NT * (b + 1))
                    link(V.tensor_copy(nmp[:, b % 2, :, 0], m))
                    V.tensor_tensor(nmp[:, b % 2, :, 1], m, nmp[:, b % 2, :, 0].bitcast(F32), ALU.subtract).then_inc(s_nmp, 1)
                elif kind == "O":
                    hf = s[2]
                    dve.wait_ge(s_ot, 2 * b + hf + 1)
                    if b and hf == 0:
                        dve.wait_ge(s_at, b)
                    o = w[:].rearrange("p (t h c) -> p t h c", t=LT, h=2 * G)
                    link(V.reciprocal(rd[:, hf], o[:, :, :, DH]))
                    V.tensor_tensor(an[:, :, hf], o[:, :, :, 0:DH],
                                    rd[:, hf][:, :, :, None].to_broadcast([P, LT, 2 * G, DH]), ALU.mult).then_inc(s_an, 1)
                elif kind == "W":
                    dve.wait_ge(s_wo, b + 1)
                    dve.wait_ge(s_xb, b + 1)
                    V.tensor_tensor(x2[:, b], w[:].rearrange("p (t d) -> p t d", t=LT), xb[:, b], ALU.add).then_inc(s_x2, 1)
                    dve.wait_ge(s_x2, b + 1)
                    for t in range(LT):
                        ins = V.bn_stats(stat2[:, t, :], x2[:, b, t, :])
                    link(ins)
                    for t in range(LT):
                        ins = V.bn_aggr(mv2[:, t, :], stat2[:, t, :])
                    link(ins)
                    if b:
                        dve.wait_ge(s_rstd2, b)
                    V.tensor_scalar(ve2[:], mv2[:, :, 1], EPS, None, ALU.add).then_inc(s_stat2, 1)
                elif kind == "Y":
                    dve.wait_ge(s_rstd2, b + 1)
                    dve.wait_ge(s_stat2, b + 1)
                    for t in range(LT):
                        ins = V.tensor_scalar(xs[:, LT * b + t, 0, 0:D], x2[:, b, t, :], mv2[:, t, 0:1], rstd2[:, t:t + 1],
                                              ALU.subtract, ALU.mult)
                    ins.then_inc(s_xs, 1)
                elif kind == "G":
                    dve.wait_ge(s_g, b + 1)
                    if b == 0:
                        dve.wait_ge(s_cst, 11)
                    V.tensor_copy(lg[:], w[:, 0:LT * E].rearrange("p (t e) -> p t e", t=LT)).then_inc(s_lg, 1)
                    dve.wait_ge(s_lg, b + 1)
                    for t in range(LT):
                        ins = V.max(top[:, t, :], lg[:, t, :])
                    link(ins)
                    if b:
                        dve.wait_ge(s_gexp, b)
                    V.tensor_tensor(gap[:], top[:, :, 1], top[:, :, 0], ALU.subtract).then_inc(s_gap, 1)
                    for t in range(LT):
                        ins = V.max_index(topi[:, t, :], top[:, t, :], lg[:, t, :])
                    link(ins)
                    link(V.tensor_copy(topf[:], topi[:, :, 0:TOPK]))
                    for k in range(TOPK):
                        ins = V.tensor_tensor(pick[:, k], topf[:, :, k:k + 1].to_broadcast([P, LT, E]),
                                              lane[:, None, :].to_broadcast([P, LT, E]), ALU.is_equal)
                    link(ins)
                    V.tensor_tensor(chosen[:], pick[:, 0], pick[:, 1], ALU.add).then_inc(s_chosen, 1)
                    dve.wait_ge(s_gexp, b + 1)
                    link(V.tensor_scalar(gden[:], gexp[:], 1.0, None, ALU.add))
                    tb = slice(LT * b, LT * b + LT)
                    link(V.reciprocal(xs[:, tb, 0, D], gden[:]))
                    V.tensor_tensor(xs[:, tb, 1, D], gexp[:], xs[:, tb, 0, D], ALU.mult)
                    V.tensor_copy(xs[:, tb, :, D + 1], ret_row[:, tb, :]).then_inc(s_prob, 1)
                elif kind == "K":
                    tb = slice(LT * b, LT * b + LT)
                    dve.wait_ge(s_rk, b + 1)
                    link(V.tensor_tensor(pos[:], w[:, 0:LT * E].rearrange("p (t e) -> p t e", t=LT),
                                         head[:, None, :].to_broadcast([P, LT, E]), ALU.add))
                    V.tensor_tensor(head[:], head[:], w[:, LT * E:LT * E + E], ALU.add).then_inc(s_pos, 1)
                    for k in range(TOPK):
                        ins = V.tensor_tensor(posk[:, k], pick[:, k], pos[:], ALU.mult)
                    link(ins)
                    for k in range(TOPK):
                        ins = V.tensor_reduce(rowf[:, k], posk[:, k], X, ALU.add)
                    link(ins)
                    V.tensor_copy(row[:, tb, :], rowf[:].rearrange("p k t -> p t k")).then_inc(s_row, 1)

            link(V.tensor_tensor(count[:], head[0:1, :], base[0:1, :], ALU.subtract))
            link(V.tensor_tensor(more[:], count[:, :, None].to_broadcast([1, E, NT]),
                                 steps128[:, None, :].to_broadcast([1, E, NT]), ALU.is_gt))
            link(V.tensor_reduce(ntile[:], more[:], X, ALU.add))
            V.tensor_scalar(skip[:], ntile[:], -1.0, float(SPAN // P), ALU.mult, ALU.add)
            link(V.tensor_tensor_scan(tile_end[:], one8[:], ntile[:], 0.0, ALU.mult, ALU.add))
            link(V.tensor_tensor(ended[:], tile_end[:, None, :].to_broadcast([1, TILES, E]),
                                 tile_no[:, :, None].to_broadcast([1, TILES, E]), ALU.is_le))
            V.tensor_reduce(expf[:], ended[:], X, ALU.add)
            link(V.tensor_tensor(skipped[:], ended[:], skip[:, None, :].to_broadcast([1, TILES, E]), ALU.mult))
            link(V.tensor_reduce(blkf[:], skipped[:], X, ALU.add))
            V.tensor_copy(pad_at[:], head[0:1, :])
            V.tensor_scalar(tile_expert[:], expf[:], float(E - 1), None, ALU.min)
            V.tensor_tensor(tile_block[:], blkf[:], tile_no[:], ALU.add).then_inc(s_tab, 1)
            for s in late:
                low_part(s[1])

            def step(t, c):
                if c + 1 <= LAST:
                    dve.wait_ge(s_eT, t + 2)
                    at_least(dve, s_up, t)
                    V.tensor_tensor(elo[:, (c + 1) % 2, :], work[0][:, 0:P], ehi[:, (c + 1) % 2, :].bitcast(F32), ALU.subtract).then_inc(s_elo, 1)
                if 0 <= c <= LAST:
                    dve.wait_ge(s_silu, t + 1)
                    dve.wait_ge(s_up, t + 1)
                    at_least(dve, s_h, t - 1)
                    V.tensor_tensor(hid[:, c % 2, :], st[:, 2 + c % 2, :], sg[:, c % 2, :], ALU.mult).then_inc(s_hid, 1)
                if c >= 2:
                    dve.wait_ge(s_d, t - 1)
                    at_least(dve, s_ret[c % 2], 8 * (t - 2 - c % 2))
                    dve.wait_ge(s_meta, t - 1)
                    V.tensor_copy(ridx[:, c % 2:c % 2 + 1], meta[:, bass.ds(t - 2, 1), 1])
                    V.tensor_scalar(ysb[:, c % 2, :], work[1][:, 0:D], meta[:, bass.ds(t - 2, 1), 0], None, ALU.mult).then_inc(s_y, 1)
                if c + 1 <= LAST:
                    dve.wait_ge(s_ld[(c + 1) % 2], 8 * (t + 1 - (c + 1) % 2) + 16)
                    V.tensor_copy(meta[:, bass.ds(t + 1, 1), :].rearrange("p a w -> p (a w)"), xt[:, (c + 1) % 2, D:D + 2]).then_inc(s_meta, 1)
            pipeline(dve, step)
            for b in range(B):
                dve.wait_ge(s_yb[b], 16)
                for k in range(TOPK):
                    V.tensor_tensor(x2[:, b], x2[:, b], yb[:, LT * b:LT * b + LT, k, :], ALU.add).then_inc(s_fin, 1)
                    dve.wait_ge(s_fin, 2 * b + k + 1)


def _layout(inputs):
    import numpy as np
    f = np.float32
    x = np.ascontiguousarray(inputs["x"])
    c = np.asarray(inputs["ctx_768"])
    ctxT = np.ones((C + 1, B * M), f)
    ctxT[:C] = c.reshape(B * M, C).T
    Wq, bq = np.asarray(inputs["L0_xattn_Wq"]), np.asarray(inputs["L0_xattn_bq"])
    Wkv, bkv = np.asarray(inputs["L0_xattn_Wkv"]), np.asarray(inputs["L0_xattn_bkv"])
    stack = np.zeros((P, 2, QD, P), f)
    wk = np.zeros((C + 1, QD, P), f); wv = np.zeros((C + 1, D), f)
    for h in range(H):
        i, g = divmod(h, G)
        for first in (ROW_HI, ROW_LO, ROW_KLO):
            r = 32 * g + first
            stack[DH * h:DH * h + DH, int(first == ROW_LO), i, r:r + DH] = np.eye(DH, dtype=f)
            wk[:C, i, r:r + DH] = Wkv[2 * DH * h:2 * DH * h + DH].T
            wk[C, i, r:r + DH] = bkv[2 * DH * h:2 * DH * h + DH]
        wk[C, i, 32 * g + ROW_MAX:32 * g + ROW_MAX + 2] = 1.0
        wv[:C, DH * h:DH * h + DH] = Wkv[2 * DH * h + DH:2 * DH * h + 2 * DH].T
        wv[C, DH * h:DH * h + DH] = bkv[2 * DH * h + DH:2 * DH * h + 2 * DH]
    low = np.zeros((P, 1), f)
    for g in range(G):
        low[32 * g + ROW_KLO:32 * g + ROW_KLO + DH, 0] = -1.0
    Wo = np.asarray(inputs["L0_xattn_Wo"])
    wo = np.zeros((D, D), f)
    for hf in range(2):
        for g in range(G):
            for j in range(2):
                h = G * (2 * hf + j) + g
                r = 64 * hf + (2 * g + j) * DH
                wo[r:r + DH] = Wo[:, DH * h:DH * h + DH].T
    bo = np.ascontiguousarray(np.broadcast_to(np.asarray(inputs["L0_xattn_bo"]), (P, D)))
    gateT = np.ascontiguousarray(np.asarray(inputs["L0_ffn_gate_w"]).T)
    wg, wu, wd = (np.asarray(inputs["L0_ffn_" + n]) for n in ("wg", "wu", "wd"))
    wgu = np.ascontiguousarray(np.concatenate([wg.transpose(0, 2, 1), wu.transpose(0, 2, 1)], axis=2))
    wdT = np.ascontiguousarray(wd.transpose(0, 2, 1).reshape(E, IC, P, D).transpose(0, 2, 1, 3).reshape(E, P, IC * D))
    return dict(x=x, ctxT=ctxT, wq=np.ascontiguousarray(Wq.T), bq=np.ascontiguousarray(bq.reshape(D, 1)), stack=stack, wk=wk, wv=wv, wo=wo, bo=bo, gateT=gateT, wgu=wgu, wd=wdT, low=low)


def kernel(**inputs):
    import concourse.bacc as _bacc
    from concourse.bass_utils import run_bass_kernel_spmd as _run

    nc = _bacc.Bacc("TRN2", target_bir_lowering=False, num_devices=1)
    arrays = _layout(inputs)
    args = {n: nc.dram_tensor(n + "_dram", a.shape, F32, kind="ExternalInput").ap() for n, a in arrays.items()}
    out = nc.dram_tensor("out_dram", (B, L, D), F32, kind="ExternalOutput").ap()
    xattn_moe(nc, out=out, **args)
    r = _run(nc, [{n + "_dram": a for n, a in arrays.items()}], core_ids=[0])
    return r.results[0]["out_dram"]
```
